# Optimizing a Trainium2 kernel written in Bass

```python
import numpy as np
import jax
import jax.numpy as jnp

def _softmax(x, axis=-1):
    return jax.nn.softmax(x, axis=axis)

def _gelu(x):
    return jax.nn.gelu(x, approximate=True)

def _silu(x):
    return jax.nn.silu(x)

def _sigmoid(x):
    return jax.nn.sigmoid(x)

def _layernorm(x, axis=-1, eps=1e-05):
    m = jnp.mean(x, axis=axis, keepdims=True)
    v = jnp.var(x, axis=axis, keepdims=True)
    return (x - m) / jnp.sqrt(v + eps)

def _scatter_add(tgt, idx, src, axis=0):
    return tgt.at[idx].add(src)

def _segment_sum(src, seg, n):
    return jax.ops.segment_sum(src, seg, n)
kernel_name = 'mk_seq_preln_d1_jaxref_r8_f91847'

def setup_inputs(seed: int=0):
    np.random.seed(seed)
    _w = jnp.asarray

    def _L0_attn_setup():
        import jax, jax.numpy as jnp
        import numpy as np
        H = 8
        LN_EPS = 1e-05
        key = jax.random.key(seed)
        ks = jax.random.split(key, 4)
        B, S, D = (4, 256, 128)
        x = jax.random.normal(ks[0], (B, S, D), dtype=jnp.float32)
        sc = 1.0 / np.sqrt(D)
        Wq = jax.random.normal(ks[1], (D, D), dtype=jnp.float32) * sc
        Wk = jax.random.normal(ks[2], (D, D), dtype=jnp.float32) * sc
        Wv = jax.random.normal(ks[3], (D, D * H), dtype=jnp.float32) * sc
        return {'x': x, 'Wq': Wq, 'bq': jnp.zeros((D,), jnp.float32), 'Wk': Wk, 'bk': jnp.zeros((D,), jnp.float32), 'Wv': Wv, 'bv': jnp.zeros((D * H,), jnp.float32), 'gamma': jnp.ones((D,), jnp.float32), 'beta': jnp.zeros((D,), jnp.float32)}
    _L0_attn_in = _L0_attn_setup()

    def _L0_ffn_setup():
        import jax, jax.numpy as jnp
        import numpy as np
        E = 8
        TOP_K = 2
        D = 128
        DFF = 4 * D
        key = jax.random.key(seed)
        ks = jax.random.split(key, 6)
        b, s = (4, 128)
        x = jax.random.normal(ks[0], (b, s, D), dtype=jnp.float32)
        centroids = jax.random.normal(ks[1], (E, D), dtype=jnp.float32)
        W1 = jax.random.normal(ks[2], (E, D, DFF), dtype=jnp.float32) * (1.0 / np.sqrt(D))
        b1 = jax.random.normal(ks[3], (E, DFF), dtype=jnp.float32) * 0.01
        W2 = jax.random.normal(ks[4], (E, DFF, D), dtype=jnp.float32) * (1.0 / np.sqrt(DFF))
        b2 = jax.random.normal(ks[5], (E, D), dtype=jnp.float32) * 0.01
        return {'x': x, 'centroids': centroids, 'W1': W1, 'b1': b1, 'W2': W2, 'b2': b2}
    _L0_ffn_in = _L0_ffn_setup()
    _d = {'L0_attn_x': _L0_attn_in['x'], 'L0_attn_Wq': _L0_attn_in['Wq'], 'L0_attn_bq': _L0_attn_in['bq'], 'L0_attn_Wk': _L0_attn_in['Wk'], 'L0_attn_bk': _L0_attn_in['bk'], 'L0_attn_Wv': _L0_attn_in['Wv'], 'L0_attn_bv': _L0_attn_in['bv'], 'L0_attn_gamma': _L0_attn_in['gamma'], 'L0_attn_beta': _L0_attn_in['beta'], 'L0_ffn_centroids': _L0_ffn_in['centroids'], 'L0_ffn_W1': _L0_ffn_in['W1'], 'L0_ffn_b1': _L0_ffn_in['b1'], 'L0_ffn_W2': _L0_ffn_in['W2'], 'L0_ffn_b2': _L0_ffn_in['b2']}
    _x0 = _d['L0_attn_x']
    _d['L0_attn_x'] = jax.random.normal(jax.random.fold_in(jax.random.key(seed), 1), (32, 256, 128), dtype=_x0.dtype)
    del _x0
    return _d

def reference(L0_attn_x, L0_attn_Wq, L0_attn_bq, L0_attn_Wk, L0_attn_bk, L0_attn_Wv, L0_attn_bv, L0_attn_gamma, L0_attn_beta, L0_ffn_centroids, L0_ffn_W1, L0_ffn_b1, L0_ffn_W2, L0_ffn_b2):

    def _L0_attn_ref(x, Wq, bq, Wk, bk, Wv, bv, gamma, beta):
        import jax, jax.numpy as jnp
        import numpy as np
        H = 8
        LN_EPS = 1e-05
        B, S, D = x.shape
        dk = D // H
        mu = jnp.mean(x, axis=-1, keepdims=True)
        var = jnp.mean(jnp.square(x - mu), axis=-1, keepdims=True)
        xn = (x - mu) * jax.lax.rsqrt(var + LN_EPS) * gamma + beta
        q = (xn @ Wq + bq).reshape(B, S, H, dk).transpose(0, 2, 1, 3)
        k = (xn @ Wk + bk).reshape(B, S, H, dk).transpose(0, 2, 1, 3)
        v = (xn @ Wv + bv).reshape(B, S, H, D).transpose(0, 2, 1, 3)
        scores = jnp.einsum('bhsd,bhtd->bhst', q, k) / jnp.sqrt(jnp.asarray(dk, x.dtype))
        p = jax.nn.softmax(scores, axis=-1)
        att = jnp.einsum('bhst,bhtd->bhsd', p, v)
        out = att.reshape(S, B, D, H).sum(axis=-1).reshape(B, S, D)
        return out

    def _L0_ffn_ref(x, centroids, W1, b1, W2, b2):
        import jax, jax.numpy as jnp
        import numpy as np
        E = 8
        TOP_K = 2
        D = 128
        DFF = 4 * D
        b, s, d = x.shape
        u = x.reshape(b * s, d)
        n = u.shape[0]
        gates = jax.nn.sigmoid(u @ centroids.T)
        if TOP_K < E:
            topk_vals, topk_idx = jax.lax.top_k(gates, TOP_K)
            mask = jnp.zeros_like(gates).at[jnp.arange(n)[:, None], topk_idx].set(topk_vals)
            gates = mask / jnp.sum(mask, axis=-1, keepdims=True)
        h = jax.nn.gelu(jnp.einsum('nd,edf->enf', u, W1) + b1[:, None, :], approximate=False)
        outs = jnp.einsum('enf,efd->end', h, W2) + b2[:, None, :]
        out = jnp.einsum('ne,end->nd', gates, outs)
        return out.reshape(b, s, d)
    x = L0_attn_x
    x = x + _L0_attn_ref(_layernorm(x, axis=-1), L0_attn_Wq, L0_attn_bq, L0_attn_Wk, L0_attn_bk, L0_attn_Wv, L0_attn_bv, L0_attn_gamma, L0_attn_beta)
    x = x + _L0_ffn_ref(_layernorm(x, axis=-1), L0_ffn_centroids, L0_ffn_W1, L0_ffn_b1, L0_ffn_W2, L0_ffn_b2)
    return x

_drawn_inputs = setup_inputs


def setup_inputs(seed=0):
    import zlib

    import numpy as np

    out = dict(_drawn_inputs(seed))
    spreads = {'L0_attn_bq': (0.0, 0.1),
     'L0_attn_bk': (0.0, 0.8),
     'L0_attn_bv': (0.0, 0.1),
     'L0_attn_gamma': (1.0, 0.2),
     'L0_attn_beta': (0.0, 0.1)}
    factors = {'L0_ffn_b1': 8.0, 'L0_ffn_b2': 8.0}
    for name, (base, spread) in spreads.items():
        noise = np.random.default_rng([zlib.crc32(name.encode()), seed]).standard_normal(out[name].shape)
        drawn = base * np.exp(spread * noise) if base else spread * noise
        out[name] = jnp.asarray(drawn.astype(out[name].dtype))
    for name, factor in factors.items():
        out[name] = (out[name] * factor).astype(out[name].dtype)
    return out
```

```python
from contextlib import ExitStack

import concourse.bass as bass
from concourse import mybir

ALU = mybir.AluOpType
ACT = mybir.ActivationFunctionType
AX = mybir.AxisListType
F32 = mybir.dt.float32
F32R = mybir.dt.float32r
BF16 = mybir.dt.bfloat16
I32 = mybir.dt.int32

P = 128
B, S, D = 32, 256, 128
H = 8
DK = D // H
EPS = 1e-5
TILES = B * S // P
PAIR = 2
RING = 4
M_ROW = 96

E = 8
DFF = 4 * D
FC = DFF // P
TOP_K = 2
SLOTS = 512
ROWS = B * S
REGION = ROWS + SLOTS
FFN_TILES = (ROWS * TOP_K + E * (SLOTS - 1)) // SLOTS
WIDTH = D + 2


def build(nc, x_in, Wq, bq, Wk, bk, Wv, bv, gamma, beta, cent, W1, b1, W2, b2, out):
    with ExitStack() as ctx:
        def sb(name, shape, dt=F32):
            return ctx.enter_context(nc.sbuf_tensor(name, shape, dt))

        def sem(name):
            return ctx.enter_context(nc.semaphore(name))

        X1 = sb("X1", [P, TILES, D])
        q_stack = [sb(f"q_stack{n}", [P, H, S], F32R) for n in range(RING)]
        k_stack = [sb(f"k_stack{n}", [P, H, S], F32R) for n in range(RING)]
        probs = [sb(f"probs{n}", [P, H, 2, S]) for n in range(2)]
        v_aug = [sb(f"v_aug{n}", [P, 4, H, 32]) for n in range(2)]
        q_hi = [sb(f"q_hi{n}", [P, 512], F32R) for n in range(2)]
        q_lo = [sb(f"q_lo{n}", [P, 512], F32R) for n in range(2)]
        k_hi = [sb(f"k_hi{n}", [P, 512], F32R) for n in range(2)]
        k_lo = [sb(f"k_lo{n}", [P, 512], F32R) for n in range(2)]
        xnT = [sb(f"xnT{n}", [P, 512]) for n in range(2)]
        z = sb("z", [P, 4, D])
        row_max = [sb(f"row_max{n}", [P, 2, H]) for n in range(2)]
        neg_maxT = [sb(f"neg_maxT{n}", [H, S], F32R) for n in range(2)]
        att = [sb(f"att{n}", [P, 2, 8, 32]) for n in range(2)]
        rden = [sb(f"rden{n}", [P, 2, 8]) for n in range(2)]
        att_n = [sb(f"att_n{n}", [P, 2, 8, DK]) for n in range(2)]
        bn = sb("bn", [P, 4, 6])
        mv = sb("mv", [P, 4, 2])
        var_e = sb("var_e", [P, 4])
        rstd = sb("rstd", [P, 4])
        minus_half = sb("minus_half", [P, 4])
        ident = sb("ident", [P, P])
        Wq_raw = sb("Wq_raw", [P, D])
        Wk_raw = sb("Wk_raw", [P, D])
        Wq_p = sb("Wq_p", [P, D])
        Wk_p = sb("Wk_p", [P, D])
        Wv_raw = sb("Wv_raw", [P, D * H])
        Wv_s = sb("Wv_s", [P, D])
        bv_raw = sb("bv_raw", [P, D * H])
        bv_s = sb("bv_s", [P, D])
        bq_c = sb("bq_c", [P, 1])
        bk_c = sb("bk_c", [P, 1])
        gamma_c = sb("gamma_c", [P, 1])
        beta_c = sb("beta_c", [P, 1])

        bn2 = sb("bn2", [P, 4, 6])
        mv2 = sb("mv2", [P, 4, 2])
        var2 = sb("var2", [P, 4])
        rstd2 = sb("rstd2", [P, 4])
        y_row = [[sb(f"y_row{n}_{k}", [P, 4, WIDTH]) for k in range(TOP_K)] for n in range(2)]
        yT = sb("yT", [P, 512])
        cent_raw = sb("cent_raw", [E, D])
        centT = sb("centT", [P, E])
        expn = sb("expn", [P, 4, E])
        den = sb("den", [P, 4, E])
        sig = sb("sig", [P, 4, E])
        sig2 = sb("sig2", [P, 4, E])
        eq = sb("eq", [P, 4, E])
        key = sb("key", [P, 4, E])
        chosen = [sb(f"chosen{k}", [P, 4, E]) for k in range(TOP_K)]
        gate = [sb(f"gate{k}", [P, 4]) for k in range(TOP_K)]
        best = [sb(f"best{k}", [P, 4]) for k in range(TOP_K)]
        gate_sum = sb("gate_sum", [P, 4])
        gate_rcp = sb("gate_rcp", [P, 4])
        picked = sb("picked", [P, 5, E], BF16)
        before = sb("before", [P, P], BF16)
        ones_bf = sb("ones_bf", [P, P], BF16)
        fill = sb("fill", [P, E])
        slot_all = sb("slot_all", [P, 4, E])
        slot_sel = [sb(f"slot_sel{k}", [P, 4, E]) for k in range(TOP_K)]
        slot_f = sb("slot_f", [P, TOP_K, 4])
        slot_idx = [sb(f"slot_idx{n}", [P, TOP_K, 4], I32) for n in range(2)]
        e_desc_i = sb("e_desc_i", [P, E], I32)
        e_desc = sb("e_desc", [P, E])
        region_i = sb("region_i", [P, E], I32)
        region = sb("region", [P, E])
        token_i = sb("token_i", [P, 4], I32)
        token = sb("token", [P, 4])
        total = sb("total", [P, E])
        tiles_i = sb("tiles_i", [P, 2, E], I32)
        tiles_f = sb("tiles_f", [P, E])
        tiles_end = sb("tiles_end", [P, E])
        ones_e = sb("ones_e", [P, E])
        tile_i = sb("tile_i", [P, FFN_TILES], I32)
        tile_n = sb("tile_n", [P, FFN_TILES])
        passed = sb("passed", [P, FFN_TILES, E])
        passed_end = sb("passed_end", [P, FFN_TILES, E])
        tile_e = sb("tile_e", [P, FFN_TILES])
        tile_start = sb("tile_start", [P, FFN_TILES])
        tile_k = sb("tile_k", [P, FFN_TILES])
        tile_row = sb("tile_row", [P, FFN_TILES])
        table = sb("table", [P, FFN_TILES, 2], I32)
        pad_start = sb("pad_start", [P, E], I32)
        pad_rows = sb("pad_rows", [P, SLOTS // P, WIDTH])
        slots = nc.dram_tensor("slots", (E * REGION + SLOTS, WIDTH), F32).ap()

        b_all = sb("b_all", [P, E, FC + 1])
        b_cur = [sb(f"b_cur{n}", [P, FC + 1]) for n in range(4)]
        tick = [sb(f"tick{n}", [P, 1]) for n in range(2)]
        gate_row = [sb(f"gate_row{n}", [P, SLOTS // P, 2]) for n in range(4)]
        y_tile = [sb(f"y_tile{n}", [P, SLOTS // P, WIDTH]) for n in range(4)]

        ps_max = [ctx.enter_context(nc.psum_tensor(f"ps_max{n}", [P, 2, S], F32)) for n in range(2)]
        ps_st = [ctx.enter_context(nc.psum_tensor(f"ps_st{n}", [P, 2, 2, S], F32)) for n in range(2)]
        ps_av = ctx.enter_context(nc.psum_tensor("ps_av", [P, 2, S], F32))
        ps_misc = ctx.enter_context(nc.psum_tensor("ps_misc", [P, 512], F32))

        w_loaded = sem("w_loaded")
        w_ready = sem("w_ready")
        const_ready = sem("const_ready")
        zeros_ready = sem("zeros_ready")
        kzeros_ready = sem("kzeros_ready")
        ones_ready = sem("ones_ready")
        x_loaded = [sem(f"x_loaded{n}") for n in range(2)]
        bn_ready = sem("bn_ready")
        mv_ready = sem("mv_ready")
        var_ready = sem("var_ready")
        rstd_ready = sem("rstd_ready")
        z_ready = sem("z_ready")
        zT_ready = sem("zT_ready")
        xnT_ready = sem("xnT_ready")
        q_proj, k_proj, v_proj = sem("q_proj"), sem("k_proj"), sem("v_proj")
        q_hi_ready, q_lo_ready = sem("q_hi_ready"), sem("q_lo_ready")
        k_hi_ready, k_lo_ready = sem("k_hi_ready"), sem("k_lo_ready")
        v_ready = sem("v_ready")
        stack_placed = [sem(f"stack_placed{n}") for n in range(RING)]
        m_placed = [sem(f"m_placed{n}") for n in range(RING)]
        smax_ready = sem("smax_ready")
        smax_reduced = sem("smax_reduced")
        maxT_ready = sem("maxT_ready")
        neg_maxT_ready = sem("neg_maxT_ready")
        st_ready = sem("st_ready")
        exp_done = sem("exp_done")
        av_done = sem("av_done")
        att_ready = sem("att_ready")
        rden_ready = sem("rden_ready")
        att_n_ready = sem("att_n_ready")
        x1_ready = sem("x1_ready")
        stored = sem("stored")

        x1_stored = sem("x1_stored")
        b_loaded = sem("b_loaded")
        tabling, table_ready = sem("tabling"), sem("table_ready")
        padded = sem("padded")
        y_loaded = [sem(f"y_loaded{n}") for n in range(4)]
        w1_loaded = [sem(f"w1_loaded{n}") for n in range(2)]
        w2_loaded = [sem(f"w2_loaded{n}") for n in range(2)]
        w1_hi_ready, w1_lo_ready = sem("w1_hi_ready"), sem("w1_lo_ready")
        w2_hi_ready, w2_lo_ready = sem("w2_hi_ready"), sem("w2_lo_ready")
        b_ready = sem("b_ready")
        yT2_psum, y_hi_ready, y_lo_ready = sem("yT2_psum"), sem("y_hi_ready"), sem("y_lo_ready")
        h_psum, h_f32_ready, h_hi_ready, h_lo_ready = sem("h_psum"), sem("h_f32_ready"), sem("h_hi_ready"), sem("h_lo_ready")
        o_psum, oT_ready, o_tok_psum, res_ready = sem("o_psum"), sem("oT_ready"), sem("o_tok_psum"), sem("res_ready")
        added = [sem(f"added{n}") for n in range(2)]
        ticked = sem("ticked")
        gate_row_ready = sem("gate_row_ready")
        cent_loaded = sem("cent_loaded")
        centT_psum, centT_ready = sem("centT_psum"), sem("centT_ready")
        iota_ready = sem("iota_ready")
        floats_ready = sem("floats_ready")
        route_const = sem("route_const")
        bn2_ready, mv2_ready = sem("bn2_ready"), sem("mv2_ready")
        var2_ready, rstd2_ready = sem("var2_ready"), sem("rstd2_ready")
        y_ready, y_copied = sem("y_ready"), sem("y_copied")
        yT_psum, yT_ready = sem("yT_psum"), sem("yT_ready")
        logits_ready, expn_ready = sem("logits_ready"), sem("expn_ready")
        gating = sem("gating")
        picked_ready = sem("picked_ready")
        rank_ready = sem("rank_ready")
        filled, slots_known = sem("filled"), sem("slots_known")
        scattered = [[sem(f"scattered{n}_{k}") for k in range(TOP_K)] for n in range(2)]

        N_W = 8 * 16
        GATING = 26

        def wait(eng, s, value):
            if not isinstance(value, int) or value > 0:
                eng.wait_ge(s, value)

        class Period:

            def __init__(self, i, r):
                self.i, self.r, self.fixed = i, r, isinstance(i, int)
                self.odd = r % 2 == 1

            def batch(self, lag):
                o = self.r - lag
                b = self.i * 4 + o
                if self.fixed and not 0 <= b < B:
                    return None
                return b, self.i + o // 4, o % 4

            def pair(self, lead):
                o = self.r + lead
                assert o % 2 == 0
                n = self.i * 2 + o // 2
                if self.fixed and not 0 <= n < B // 2:
                    return None
                return n, (o // 2) % 2

        def same_parity(t, lead):
            return t.i + (t.r + lead) // 4

        def periods(eng, body):
            for j in range(-3, 12):
                body(Period(j // 4, j % 4))
            with eng.Fori(3, 7) as i:
                for r in range(4):
                    body(Period(i, r))
            for j in range(28, 42):
                body(Period(j // 4, j % 4))

        def cols(t, first, count):
            pattern = "p h t s -> p (h t s)" if len(t.shape) == 4 else "p h s -> p (h s)"
            return t[:].rearrange(pattern)[:, first * 512:(first + count) * 512]

        w1_raw = [cols(probs[0], n, 1) for n in range(2)]
        w2_raw = [cols(probs[0], 2 + n, 1) for n in range(2)]
        h_f32 = [cols(probs[1], n, 1) for n in range(2)]
        oT = [cols(probs[1], 2 + n, 1) for n in range(2)]
        res = [cols(probs[1], 4 + n, 1) for n in range(2)]
        w1_hi = [cols(q_stack[0], n, 1) for n in range(2)]
        w2_hi = [cols(q_stack[0], 2 + n, 1) for n in range(2)]
        w1_lo = [cols(q_stack[1], n, 1) for n in range(2)]
        w2_lo = [cols(q_stack[1], 2 + n, 1) for n in range(2)]
        y_hi = [cols(q_stack[2], n, 1) for n in range(2)]
        y_lo = [cols(q_stack[2], 2 + n, 1) for n in range(2)]
        h_hi = [[cols(k_stack[n], f, 1) for f in range(FC)] for n in range(2)]
        h_lo = [[cols(k_stack[2 + n], f, 1) for f in range(FC)] for n in range(2)]
        ps_h = [ps_st[f // 2][:, f % 2, :, :].rearrange("p a s -> p (a s)") for f in range(FC)]
        ps_o = [ps_max[n][:].rearrange("p a s -> p (a s)") for n in range(2)]
        ps_y = ps_av[:].rearrange("p a s -> p (a s)")
        ps_t = ps_misc[:]

        class Step:

            def __init__(self, i, r):
                self.i, self.r, self.fixed = i, r, isinstance(i, int)

            def tile(self, lead):
                o = self.r + lead
                n = self.i * 4 + o
                if self.fixed and not 0 <= n < FFN_TILES:
                    return None
                return n, self.i + o // 4, o % 4

        def steps(eng, body):
            last = (FFN_TILES - 3) // 4
            for t in range(-2, 4):
                body(Step(t // 4, t % 4))
            with eng.Fori(1, last) as i:
                for r in range(4):
                    body(Step(i, r))
            for t in range(4 * last, FFN_TILES + 2):
                body(Step(t // 4, t % 4))

        def since(n, back):
            return not isinstance(n, int) or n >= back

        def loads(i, r, ring):
            return 16 * (i + 1) if ring == 4 else 16 * (i * 2 + r // 2 + 1)

        block = ctx.enter_context(nc.Block())

        @block.sync
        def _(sp):
            xt = x_in.rearrange("b (c p) d -> p (b c) d", p=P)
            out_t = out.rearrange("b (c p) d -> p (b c) d", p=P)

            def load_x(n, par):
                sp.dma_start(X1[:, bass.ds(n * 4, 4), :], xt[:, bass.ds(n * 4, 4), :]).then_inc(x_loaded[par], 16)

            load_x(0, 0)
            sp.dma_start(gamma_c[:], gamma.rearrange("(p o) -> p o", o=1)).then_inc(w_loaded, 16)
            sp.dma_start(beta_c[:], beta.rearrange("(p o) -> p o", o=1)).then_inc(w_loaded, 16)
            sp.dma_start(Wq_raw[:], Wq).then_inc(w_loaded, 16)
            sp.dma_start(Wk_raw[:], Wk).then_inc(w_loaded, 16)
            sp.dma_start(bq_c[:], bq.rearrange("(h d o) -> d h o", h=H, o=1), allow_slow_non_contiguous=True).then_inc(w_loaded, 16)
            sp.dma_start(bk_c[:], bk.rearrange("(h d o) -> d h o", h=H, o=1), allow_slow_non_contiguous=True).then_inc(w_loaded, 16)
            sp.dma_start(Wv_raw[:], Wv).then_inc(w_loaded, 16)
            sp.dma_start(bv_raw[:], bv.rearrange("(o n) -> o n", o=1).broadcast_to([P, D * H])).then_inc(w_loaded, 16)
            load_x(1, 1)

            def body(t):
                if not t.odd:
                    p = t.pair(4)
                    if p and not (t.fixed and p[0] < 2):
                        wait(sp, bn_ready, 4 * (p[0] - 1))
                        load_x(*p)
                nb = t.batch(-1)
                if nb:
                    b, bi, slot = nb
                    n = bi * 2 + slot // 2
                    par = (slot // 2) % 2
                    wait(sp, q_lo_ready, n + 1)
                    wait(sp, k_lo_ready, n + 1)
                    wait(sp, st_ready, 4 * b - 12)
                    half = slice((slot % 2) * S, (slot % 2) * S + S)
                    for part, (qs, ks) in enumerate(((q_hi, k_hi), (q_lo, k_hi), (q_hi, k_lo))):
                        for stack, src in ((q_stack, qs), (k_stack, ks)):
                            sp.dma_start(
                                stack[slot][part * DK:(part + 1) * DK, :, :].rearrange("p h s -> p (h s)").bitcast(F32),
                                src[par][:, half].bitcast(F32)).then_inc(stack_placed[slot], 16)
                nb = t.batch(4)
                if nb:
                    b = nb[0]
                    wait(sp, x1_ready, b + 1)
                    sp.dma_start(out_t[:, bass.ds(b * 2, 2), :], X1[:, bass.ds(b * 2, 2), :]).then_inc(x1_stored, 16)

            sp.dma_start(cent_raw[:], cent).then_inc(cent_loaded, 16)
            for f in range(FC):
                sp.dma_start(b_all[:, :, f:f + 1], b1.rearrange("e (f p o) -> f p e o", p=P, o=1)[f],
                             allow_slow_non_contiguous=True).then_inc(b_loaded, 16)
            sp.dma_start(b_all[:, :, FC:FC + 1], b2.rearrange("e (p o) -> p e o", o=1),
                         allow_slow_non_contiguous=True).then_inc(b_loaded, 16)
            sp.wait_ge(zeros_ready, 1)
            sp.wait_ge(kzeros_ready, 1)
            periods(sp, body)
            for n in range(2):
                for k in range(TOP_K):
                    sp.wait_ge(scattered[n][k], 64 * B // 4)
            sp.wait_ge(table_ready, 1)
            tiled = slots.rearrange("(c p) w -> p c w", p=P)
            sp.dma_start(tiled[:, E * REGION // P:, :], pad_rows[:]).then_inc(padded, 16)
            for e in range(E):
                start = sp.value_load(pad_start[0:1, e:e + 1], min_val=e * REGION, max_val=e * REGION + ROWS)
                sp.dma_start(slots[bass.ds(start, SLOTS), :].rearrange("(c p) w -> p c w", p=P),
                             pad_rows[:]).then_inc(padded, 16)

            def load(t):
                if t.tile(2):
                    n, i, r = t.tile(2)
                    e = sp.value_load(table[0:1, bass.ds(n, 1), 1:2].rearrange("p a b -> p (a b)"), min_val=0, max_val=E - 1)
                    row = sp.value_load(table[0:1, bass.ds(n, 1), 0:1].rearrange("p a b -> p (a b)"), min_val=0, max_val=E * REGION)
                    if not since(n, 1):
                        sp.wait_ge(padded, 16 * (E + 1))
                    if since(n, 4):
                        sp.wait_ge(yT2_psum, n - 3)
                        sp.wait_ge(gate_row_ready, n - 3)
                    sp.dma_start(y_tile[r][:], slots[bass.ds(row, SLOTS), :].rearrange("(c p) w -> p c w", p=P)).then_inc(y_loaded[r], 16)
                    if since(n, 2):
                        sp.wait_ge(w1_lo_ready, n - 1)
                    sp.dma_start(w1_raw[r % 2], W1[bass.ds(e, 1), :, :].rearrange("e d f -> d (e f)")).then_inc(w1_loaded[r % 2], 16)
                if t.tile(1):
                    n, i, r = t.tile(1)
                    e = sp.value_load(table[0:1, bass.ds(n, 1), 1:2].rearrange("p a b -> p (a b)"), min_val=0, max_val=E - 1)
                    if since(n, 2):
                        sp.wait_ge(w2_lo_ready, n - 1)
                    sp.dma_start(w2_raw[r % 2].rearrange("p (f d) -> p f d", f=FC),
                                 W2[bass.ds(e, 1), :, :].rearrange("e (f p) d -> p (e f) d", p=P)).then_inc(w2_loaded[r % 2], 16)

            steps(sp, load)

        @block.gpsimd
        def _(pool):
            pool.memset(minus_half[:], -0.5).then_inc(const_ready, 1)
            pool.memset(ident[:], 0.0).then_inc(const_ready, 1)
            for n in range(RING):
                pool.memset(k_stack[n][:].bitcast(F32), 0.0)
            for n in range(2):
                last = pool.memset(v_aug[n][:], 0.0)
            last.then_inc(kzeros_ready, 1)
            pool.wait_ge(kzeros_ready, 1)
            for n in range(RING):
                last = pool.memset(k_stack[n][M_ROW:M_ROW + 1, :, :].bitcast(F32), 1.0)
            last.then_inc(kzeros_ready, 1)
            pool.wait_ge(kzeros_ready, 2)
            for n in range(2):
                last = pool.memset(v_aug[n][:, :, :, DK:DK + 1], 1.0)
            last.then_inc(ones_ready, 1)
            pool.iota(e_desc_i[:], pattern=[[-1, E]], base=E, channel_multiplier=0).then_inc(iota_ready, 1)
            pool.iota(region_i[:], pattern=[[REGION, E]], base=0, channel_multiplier=0).then_inc(iota_ready, 1)
            pool.iota(token_i[:], pattern=[[P, 4]], base=0, channel_multiplier=1).then_inc(iota_ready, 1)
            pool.iota(tile_i[:], pattern=[[1, FFN_TILES]], base=0, channel_multiplier=0).then_inc(iota_ready, 1)
            pool.memset(ones_bf[:], 1.0).then_inc(route_const, 1)
            pool.memset(ones_e[:], 1.0).then_inc(route_const, 1)
            pool.memset(picked[:], 0.0).then_inc(route_const, 1)
            pool.memset(pad_rows[:], 0.0).then_inc(route_const, 1)
            pool.memset(tick[0][:], 0.0).then_inc(route_const, 1)
            pool.wait_ge(route_const, 5)
            pool.affine_select(out=before[:], in_=ones_bf[:], compare_op=ALU.is_gt, fill=0.0, base=0,
                               pattern=[[1, P]], channel_multiplier=-1).then_inc(route_const, 1)
            pool.memset(pad_rows[:, :, D + 1].bitcast(I32), 2 * ROWS).then_inc(route_const, 1)
            pool.wait_ge(const_ready, 2)
            pool.affine_select(out=ident[:], in_=ident[:], compare_op=ALU.not_equal, fill=1.0, base=0,
                               pattern=[[-1, P]], channel_multiplier=1).then_inc(const_ready, 1)

            def body(t):
                if t.odd:
                    p = t.pair(3)
                    if p:
                        n = p[0]
                        wait(pool, var_ready, n + 1)
                        wait(pool, z_ready, n)
                        pool.tensor_tensor(rstd[:], var_e[:], minus_half[:], ALU.pow).then_inc(rstd_ready, 1)
                k, pr = (1, t.pair(-11)) if t.odd else (0, t.pair(-10))
                if pr:
                    wait(pool, slots_known, pr[0] + 1)
                nb = t.batch(3)
                if nb:
                    b, bi, slot = nb
                    par = slot % 2
                    wait(pool, rden_ready, b + 1)
                    pool.tensor_tensor(att_n[par][:], att[par][:, :, :, 0:DK],
                                       rden[par][:].unsqueeze(3).to_broadcast([P, 2, 8, DK]),
                                       ALU.mult).then_inc(att_n_ready, 1)
                    wait(pool, att_n_ready, b + 1)
                    xs = X1[:, bass.ds(b * 2, 2), :]
                    pool.tensor_tensor(xs, xs, att_n[par][:].rearrange("p g m d -> p g (m d)"),
                                       ALU.add).then_inc(x1_ready, 1)
                if pr:
                    n, par_s = pr
                    for c in range(4):
                        pool.indirect_dma_start(slots, bass.IndirectOffsetOnAxis(slot_idx[par_s][:, k, c:c + 1], 0),
                                                y_row[par_s][k][:, c, :], None).then_inc(scattered[par_s][k], 16)
                p = t.pair(-5) if t.odd else None
                if p:
                    n = p[0]
                    wait(pool, var2_ready, n + 1)
                    wait(pool, y_ready, n)
                    pool.tensor_tensor(rstd2[:], var2[:], minus_half[:], ALU.pow).then_inc(rstd2_ready, 1)

            periods(pool, body)
            out_rows = out.rearrange("b s d -> (b s) d")
            pool.wait_ge(table_ready, 1)

            pool.wait_ge(x1_stored, 16 * B)
            last_row = pool.to_reg(ROWS - 1)

            def expert(t):
                if t.tile(1):
                    n, i, r = t.tile(1)
                    e = pool.value_load(table[0:1, bass.ds(n, 1), 1:2].rearrange("p a b -> p (a b)"), min_val=0, max_val=E - 1)
                    if since(n, 4):
                        pool.wait_ge(oT_ready, n - 3)
                    pool.wait_ge(b_loaded, 16 * (FC + 1))
                    pool.tensor_copy(b_cur[r][:], b_all[:, bass.ds(e, 1), :].rearrange("p a b -> p (a b)")).then_inc(b_ready, 1)
                if t.tile(0):
                    n, i, r = t.tile(0)
                    pool.wait_ge(w2_hi_ready, n + 1)
                    if since(n, 2):
                        pool.wait_ge(o_psum, n - 1)
                    pool.tensor_tensor(w2_lo[r % 2], w2_raw[r % 2], w2_hi[r % 2].bitcast(F32), ALU.subtract).then_inc(w2_lo_ready, 1)
                if t.tile(-2):
                    n, i, r = t.tile(-2)
                    par = r % 2
                    pool.wait_ge(res_ready, n + 1)
                    if since(n, 1):
                        o = r - 1
                        pool.wait_ge(added[o % 2], 64 * ((i + o // 4) * 2 + (o % 4) // 2 + 1))
                    pool.wait_ge(gate_row_ready, n + 1)
                    if since(n, 1):
                        pool.wait_ge(ticked, n)
                    pool.tensor_tensor(tick[1][:], tick[0][:], tick[0][:], ALU.add).then_inc(ticked, 1)
                    for c in range(SLOTS // P):
                        pool.indirect_dma_start(
                            out_rows, bass.IndirectOffsetOnAxis(gate_row[r][:, c, 1:2].bitcast(I32), 0),
                            res[par][:, c * P:(c + 1) * P], None, bounds_check=last_row, oob_is_err=False,
                            compute_op=ALU.add).then_inc(added[par], 16)

            steps(pool, expert)
            pool.wait_ge(added[0], 64 * ((FFN_TILES + 1) // 2))
            pool.wait_ge(added[1], 64 * (FFN_TILES // 2))

        @block.scalar
        def _(act):
            act.wait_ge(w_loaded, N_W)
            act.wait_ge(centT_psum, 1)
            act.activation(centT[:], ps_misc[:, 0:E], ACT.Copy).then_inc(centT_ready, 1)
            act.activation(Wq_p[:].rearrange("p (d h) -> p d h", h=H),
                           Wq_raw[:].rearrange("p (h d) -> p d h", h=H), ACT.Copy).then_inc(w_ready, 1)
            act.activation(Wk_p[:].rearrange("p (d h) -> p d h", h=H),
                           Wk_raw[:].rearrange("p (h d) -> p d h", h=H), ACT.Copy).then_inc(w_ready, 1)

            def exps(t, hp):
                nb = t.batch(2)
                if nb:
                    b, bi, slot = nb
                    if hp == 0:
                        wait(act, av_done, 2 * b - 2)
                    wait(act, st_ready, 4 * b + hp + 1)
                    act.activation(probs[slot % 2][:, 2 * hp:2 * hp + 2, :, :], ps_st[hp % 2][:], ACT.Exp,
                                   scale=DK ** -0.5).then_inc(exp_done, 1)

            def body(t):
                nb = t.batch(1)
                if nb:
                    b, bi, slot = nb
                    par = slot % 2
                    wait(act, maxT_ready, b + 1)
                    if not (t.fixed and b < 2):
                        o = slot - 2
                        act.wait_ge(m_placed[o % 4], 16 * (bi + o // 4 + 1))
                    act.activation(neg_maxT[par][:], ps_misc[0:H, 0:S], ACT.Copy, scale=-1.0).then_inc(neg_maxT_ready, 1)
                exps(t, 0)
                if nb:
                    wait(act, neg_maxT_ready, b + 1)
                    act.wait_ge(stack_placed[slot], 96 * (bi + 1))
                    act.dma_start(q_stack[slot][M_ROW:M_ROW + 1, :, :].rearrange("p h s -> p (h s)").bitcast(F32),
                                  neg_maxT[par][:].bitcast(F32)).then_inc(m_placed[slot], 16)
                p = None if t.odd else t.pair(2)
                if p:
                    n, par = p
                    wait(act, zT_ready, n + 1)
                    wait(act, v_proj, n - 1)
                    act.activation(xnT[par][:], ps_misc[:], ACT.Identity, bias=beta_c[:, 0:1],
                                   scale=gamma_c[:, 0:1]).then_inc(xnT_ready, 1)
                exps(t, 1)
                pr = t.pair(-7) if t.odd else None
                if pr:
                    ny, py = pr
                    wait(act, yT_psum, ny + 1)
                    act.activation(yT[:], ps_misc[:], ACT.Copy).then_inc(yT_ready, 1)
                    wait(act, y_ready, ny + 1)
                    if not (t.fixed and ny < 2):
                        act.wait_ge(scattered[py][1], 64 * same_parity(t, -7))
                    act.activation(y_row[py][1][:, :, 0:D], y_row[py][0][:, :, 0:D], ACT.Copy).then_inc(y_copied, 1)
                if p:
                    wait(act, q_proj, n + 1)
                    if not (t.fixed and n < 2):
                        for o in (t.r + 2 - 4, t.r + 2 - 3):
                            act.wait_ge(stack_placed[o % 4], 96 * (t.i + o // 4 + 1))
                    act.activation(q_hi[par][:], ps_misc[:], ACT.Identity, bias=bq_c[:, 0:1]).then_inc(q_hi_ready, 1)
                exps(t, 2)
                exps(t, 3)
                if p:
                    wait(act, k_proj, n + 1)
                    act.activation(k_hi[par][:], ps_misc[:], ACT.Identity, bias=bk_c[:, 0:1]).then_inc(k_hi_ready, 1)
                if pr:
                    wait(act, logits_ready, ny + 1)
                    wait(act, gating, GATING * ny)
                    act.activation(expn[:], ps_misc[:, 0:4 * E].rearrange("p (c e) -> p c e", e=E), ACT.Exp,
                                   scale=-1.0).then_inc(expn_ready, 1)

            periods(act, body)
            act.wait_ge(table_ready, 1)

            def hidden(t, f):
                if t.tile(0):
                    n, i, r = t.tile(0)
                    par = r % 2
                    if f == 0:
                        act.wait_ge(b_ready, n + 1)
                    act.wait_ge(h_psum, 4 * n + f + 1)
                    if not (t.fixed and 4 * n + f < 2):
                        act.wait_ge(h_lo_ready, 4 * n + f - 1)
                    act.activation(h_f32[f % 2], ps_h[f], ACT.Gelu, bias=b_cur[r][:, f:f + 1]).then_inc(h_f32_ready, 1)
                    if f == 0 and since(n, 2):
                        act.wait_ge(o_psum, n - 1)
                    act.activation(h_hi[par][f], ps_h[f], ACT.Gelu, bias=b_cur[r][:, f:f + 1]).then_inc(h_hi_ready, 1)

            def body_b(t):
                hidden(t, 0)
                hidden(t, 1)
                hidden(t, 2)
                if t.tile(1):
                    n, i, r = t.tile(1)
                    act.wait_ge(yT2_psum, n + 1)
                    act.activation(y_hi[r % 2], ps_y, ACT.Copy).then_inc(y_hi_ready, 1)
                hidden(t, 3)

            steps(act, body_b)

        @block.tensor
        def _(pe):
            pe.wait_ge(const_ready, 3)
            pe.wait_ge(cent_loaded, 16)
            pe.transpose(ps_misc[:, 0:E], cent_raw[:], ident[0:E, 0:E]).then_inc(centT_psum, 1)
            pe.wait_ge(centT_ready, 1)
            pe.wait_ge(ones_ready, 1)
            pe.wait_ge(w_ready, 4)
            pe.wait_ge(route_const, 7)

            def max_unit(t, k):
                nb = t.batch(0)
                if nb:
                    b, bi, slot = nb
                    if k == 0:
                        pe.wait_ge(stack_placed[slot], 96 * (bi + 1))
                    sc, hp = k // 4, k % 4
                    wait(pe, smax_reduced, 8 * b + k - 1)
                    for hh in range(2):
                        h = 2 * hp + hh
                        last = pe.matmul(ps_max[k % 2][:, hh, :], q_stack[slot][0:M_ROW, h, sc * P:(sc + 1) * P],
                                         k_stack[slot][0:M_ROW, h, :], start=True, stop=True)
                    last.then_inc(smax_ready, 1)

            def st_unit(t, h):
                nb = t.batch(2)
                if nb:
                    b, bi, slot = nb
                    if h == 0:
                        pe.wait_ge(m_placed[slot], 16 * (bi + 1))
                    hp = h // 2
                    if h % 2 == 0:
                        wait(pe, exp_done, 4 * b + hp - 1)
                    for tc in range(2):
                        last = pe.matmul(ps_st[hp % 2][:, h % 2, tc, :], k_stack[slot][:, h, tc * P:(tc + 1) * P],
                                         q_stack[slot][:, h, :], start=True, stop=True)
                    if h % 2 == 1:
                        last.then_inc(st_ready, 1)

            def av(t, lag, g):
                nb = t.batch(lag)
                if nb:
                    b, bi, slot = nb
                    n = bi * 2 + slot // 2
                    if g == 0:
                        wait(pe, v_ready, n + 1)
                        wait(pe, att_ready, b)
                    wait(pe, exp_done, 4 * b + 2 * g + 2)
                    for tc in range(2):
                        for j in range(4):
                            h = 4 * g + j
                            last = pe.matmul(ps_av[32 * j:32 * j + 32, g, :],
                                             v_aug[(slot // 2) % 2][:, 2 * (slot % 2) + tc, h, :],
                                             probs[slot % 2][:, h, tc, :], start=(tc == 0), stop=(tc == 1),
                                             tile_position=(0, 32 * j))
                    last.then_inc(av_done, 1)

            def body(t):
                p = None if t.odd else t.pair(2)
                pv = t.pair(-1) if t.odd else None
                for k in range(8):
                    max_unit(t, k)
                    if k == 0 and t.batch(1):
                        b, bi, slot = t.batch(1)
                        wait(pe, smax_reduced, 8 * b + 8)
                        if t.odd:
                            if t.pair(1):
                                wait(pe, k_hi_ready, t.pair(1)[0] + 1)
                                wait(pe, k_lo_ready, t.pair(1)[0] + 1)
                        else:
                            if t.pair(-2):
                                wait(pe, v_ready, t.pair(-2)[0] + 1)
                            if t.pair(-8):
                                wait(pe, expn_ready, t.pair(-8)[0] + 1)
                        for sc in range(2):
                            last = pe.transpose(ps_misc[0:H, sc * P:(sc + 1) * P], row_max[slot % 2][:, sc, :], ident[:])
                        last.then_inc(maxT_ready, 1)
                    if k == 1 and t.odd and t.pair(-9):
                        wait(pe, picked_ready, t.pair(-9)[0] + 1)
                        if t.batch(1):
                            wait(pe, neg_maxT_ready, t.batch(1)[0] + 1)
                        rank = ps_misc[:, 0:5 * E]
                        pe.matmul(rank, before[:], picked[:].rearrange("p c e -> p (c e)"), start=True, stop=False)
                        for c in range(4):
                            last = pe.matmul(rank[:, (c + 1) * E:5 * E], ones_bf[:],
                                             picked[:, c:c + 1, :].to_broadcast([P, 4 - c, E]),
                                             start=False, stop=(c == 3))
                        last.then_inc(rank_ready, 1)
                    if k == 4 and t.odd and t.pair(-7):
                        ny, py = t.pair(-7)
                        wait(pe, y_ready, ny + 1)
                        if t.pair(-1):
                            wait(pe, v_ready, t.pair(-1)[0] + 1)
                        elif t.batch(1):
                            wait(pe, neg_maxT_ready, t.batch(1)[0] + 1)
                        if t.pair(-9):
                            wait(pe, slots_known, t.pair(-9)[0] + 1)
                        for c in range(4):
                            last = pe.transpose(ps_misc[:, c * P:(c + 1) * P], y_row[py][0][:, c, 0:D], ident[:])
                        last.then_inc(yT_psum, 1)
                    if k == 6 and t.odd and t.pair(-7):
                        wait(pe, yT_ready, ny + 1)
                        for c in range(4):
                            last = pe.matmul(ps_misc[:, c * E:(c + 1) * E], yT[:, c * P:(c + 1) * P], centT[:],
                                             start=True, stop=True)
                        last.then_inc(logits_ready, 1)
                    if k == 1 and p:
                        n, par = p
                        wait(pe, z_ready, n + 1)
                        if t.batch(1):
                            wait(pe, neg_maxT_ready, t.batch(1)[0] + 1)
                        for c in range(4):
                            last = pe.transpose(ps_misc[:, c * P:(c + 1) * P], z[:, c, :], ident[:])
                        last.then_inc(zT_ready, 1)
                    if k == 3 and p:
                        wait(pe, xnT_ready, n + 1)
                        pe.matmul(ps_misc[:], Wq_p[:], xnT[par][:], start=True, stop=True).then_inc(q_proj, 1)
                    if k == 6 and p:
                        wait(pe, q_hi_ready, n + 1)
                        wait(pe, q_lo_ready, n + 1)
                        pe.matmul(ps_misc[:], Wk_p[:], xnT[par][:], start=True, stop=True).then_inc(k_proj, 1)
                    if k == 3 and pv:
                        n, par = pv
                        wait(pe, neg_maxT_ready, t.batch(1)[0] + 1)
                        if t.pair(-9):
                            wait(pe, slots_known, t.pair(-9)[0] + 1)
                        for c in range(4):
                            last = pe.matmul(ps_misc[:, c * P:(c + 1) * P], xnT[par][:, c * P:(c + 1) * P], Wv_s[:],
                                             start=True, stop=True)
                        last.then_inc(v_proj, 1)
                    st_unit(t, k)
                    if k == 2:
                        av(t, 3, 1)
                    if k == 6:
                        av(t, 2, 0)

            periods(pe, body)
            pe.wait_ge(table_ready, 1)

            def three(o, w_hi, w_lo, x_hi, x_lo, start, stop):
                pe.matmul(o, w_hi, x_hi, start=start, stop=False)
                pe.matmul(o, w_lo, x_hi, start=False, stop=False)
                return pe.matmul(o, w_hi, x_lo, start=False, stop=stop)

            def body_b(t):
                for f in range(FC):
                    part = slice(f * P, (f + 1) * P)
                    if t.tile(0):
                        n, i, r = t.tile(0)
                        par = r % 2
                        if f == 0:
                            pe.wait_ge(w1_hi_ready, n + 1)
                            pe.wait_ge(w1_lo_ready, n + 1)
                            pe.wait_ge(y_lo_ready, n + 1)
                        if since(n, 1):
                            pe.wait_ge(h_hi_ready, 4 * (n - 1) + f + 1)
                        three(ps_h[f], w1_hi[par][:, part], w1_lo[par][:, part], y_hi[par], y_lo[par],
                              True, True).then_inc(h_psum, 1)
                    if t.tile(-1):
                        n, i, r = t.tile(-1)
                        par = r % 2
                        if f == 0:
                            pe.wait_ge(w2_hi_ready, n + 1)
                            pe.wait_ge(w2_lo_ready, n + 1)
                            if since(n, 2):
                                pe.wait_ge(oT_ready, n - 1)
                        pe.wait_ge(h_lo_ready, 4 * n + f + 1)
                        last = three(ps_o[par], w2_hi[par][:, part], w2_lo[par][:, part], h_hi[par][f], h_lo[par][f],
                                     f == 0, f == FC - 1)
                        if f == FC - 1:
                            last.then_inc(o_psum, 1)
                    if f == 1 and t.tile(-2):
                        n, i, r = t.tile(-2)
                        pe.wait_ge(oT_ready, n + 1)
                        if since(n, 1):
                            pe.wait_ge(res_ready, n)
                        for c in range(SLOTS // P):
                            last = pe.transpose(ps_t[:, c * P:(c + 1) * P], oT[r % 2][:, c * P:(c + 1) * P], ident[:])
                        last.then_inc(o_tok_psum, 1)
                    if f == 1 and t.tile(1):
                        n, i, r = t.tile(1)
                        pe.wait_ge(y_loaded[r], loads(i, r, 4))
                        if since(n, 1):
                            pe.wait_ge(y_lo_ready, n)
                        for c in range(SLOTS // P):
                            last = pe.transpose(ps_y[:, c * P:(c + 1) * P], y_tile[r][:, c, 0:D], ident[:])
                        last.then_inc(yT2_psum, 1)

            steps(pe, body_b)

        @block.vector
        def _(dve):
            for n in range(RING):
                last = dve.memset(q_stack[n][:].bitcast(F32), 0.0)
            last.then_inc(zeros_ready, 1)
            dve.wait_ge(iota_ready, 4)
            for dst, src in ((e_desc, e_desc_i), (region, region_i), (fill, region_i), (token, token_i), (tile_n, tile_i)):
                dve.tensor_copy(dst[:], src[:]).then_inc(floats_ready, 1)
            dve.wait_ge(floats_ready, 5)
            dve.wait_ge(w_loaded, N_W)
            dve.tensor_reduce(Wv_s[:], Wv_raw[:].rearrange("p (n g) -> p n g", g=8), AX.X, ALU.add).then_inc(w_ready, 1)
            dve.tensor_reduce(bv_s[:], bv_raw[:].rearrange("p (n g) -> p n g", g=8), AX.X, ALU.add).then_inc(w_ready, 1)

            def reduce_unit(t, k):
                nb = t.batch(0)
                if nb:
                    b, bi, slot = nb
                    if k == 0:
                        wait(dve, maxT_ready, b - 1)
                    sc, hp = k // 4, k % 4
                    wait(dve, smax_ready, 8 * b + k + 1)
                    dve.tensor_reduce(row_max[slot % 2][:, sc, 2 * hp:2 * hp + 2], ps_max[k % 2][:], AX.X,
                                      ALU.max).then_inc(smax_reduced, 1)

            def split(n, par, src_ready, hi, lo, lo_ready, hi_ready, bias):
                wait(dve, hi_ready, n + 1)
                dve.scalar_tensor_tensor(out=lo[par][:], in0=ps_misc[:], scalar=bias[:, 0:1], in1=hi[par][:].bitcast(F32),
                                         op0=ALU.add, op1=ALU.subtract).then_inc(lo_ready, 1)

            def own(n, count):
                wait(dve, gating, GATING * n + count)

            def step(ins):
                ins.then_inc(gating, 1)

            def over_e(a):
                return a[:].unsqueeze(2).to_broadcast([P, 4, E])

            def tile_of(n, c):
                return X1[:, bass.ds(n * 4 + c, 1), :].rearrange("p o d -> p (o d)")

            def normalise_tokens(n):
                wait(dve, x1_ready, 2 * n + 2)
                for c in range(4):
                    dve.bn_stats(bn2[:, c, :], tile_of(n, c)).then_inc(bn2_ready, 1)

            def aggregate_tokens(n):
                for c in range(4):
                    last = dve.bn_aggr(mv2[:, c, :], bn2[:, c, :])
                last.then_inc(mv2_ready, 1)
                wait(dve, mv2_ready, n + 1)
                dve.tensor_scalar(var2[:], mv2[:, :, 1], EPS, None, ALU.add).then_inc(var2_ready, 1)

            def choose(n, par):
                desc = e_desc[:].unsqueeze(1).to_broadcast([P, 4, E])
                wait(dve, expn_ready, n + 1)
                step(dve.tensor_scalar(den[:], expn[:], 1.0, None, ALU.add))
                own(n, 1)
                step(dve.reciprocal(sig[:], den[:]))
                own(n, 2)
                for k, values in enumerate((sig, sig2)):
                    base = 2 + 6 * k
                    step(dve.tensor_reduce(gate[k][:], values[:], AX.X, ALU.max))
                    own(n, base + 1)
                    step(dve.tensor_tensor(eq[:], values[:], over_e(gate[k]), ALU.is_equal))
                    own(n, base + 2)
                    step(dve.tensor_tensor(key[:], eq[:], desc, ALU.mult))
                    own(n, base + 3)
                    step(dve.tensor_reduce(best[k][:], key[:], AX.X, ALU.max))
                    own(n, base + 4)
                    step(dve.tensor_tensor(chosen[k][:], desc, over_e(best[k]), ALU.is_equal))
                    own(n, base + 5)
                    step(dve.scalar_tensor_tensor(out=sig2[:], in0=chosen[k][:], scalar=-2.0, in1=values[:],
                                                  op0=ALU.mult, op1=ALU.add))
                    own(n, base + 6)
                step(dve.tensor_tensor(gate_sum[:], gate[0][:], gate[1][:], ALU.add))
                wait(dve, rank_ready, n)
                dve.tensor_tensor(picked[:, 0:4, :], chosen[0][:], chosen[1][:], ALU.add).then_inc(picked_ready, 1)
                own(n, 15)
                step(dve.reciprocal(gate_rcp[:], gate_sum[:]))
                own(n, 16)
                wait(dve, y_copied, n + 1)
                for k in range(TOP_K):
                    step(dve.tensor_tensor(y_row[par][k][:, :, D], gate[k][:], gate_rcp[:], ALU.mult))
                    step(dve.tensor_copy(y_row[par][k][:, :, D + 1].bitcast(I32), token[:]))
                own(n, 20)
                step(dve.tensor_scalar(token[:], token[:], float(4 * P), None, ALU.add))

            def place(n, par, t):
                rank = ps_misc[:, 0:5 * E].rearrange("p (c e) -> p c e", e=E)
                wait(dve, rank_ready, n + 1)
                own(n, 21)
                step(dve.tensor_tensor(slot_all[:], rank[:, 0:4, :], fill[:].unsqueeze(1).to_broadcast([P, 4, E]), ALU.add))
                own(n, 22)
                dve.tensor_tensor(fill[:], rank[:, 4, :], fill[:], ALU.add).then_inc(filled, 1)
                for k in range(TOP_K):
                    step(dve.tensor_tensor(slot_sel[k][:], slot_all[:], chosen[k][:], ALU.mult))
                own(n, 24)
                wait(dve, filled, n + 1)
                for k in range(TOP_K):
                    step(dve.tensor_reduce(slot_f[:, k, :], slot_sel[k][:], AX.X, ALU.add))
                own(n, 26)
                if not (t.fixed and n < 2):
                    for k in range(TOP_K):
                        dve.wait_ge(scattered[par][k], 64 * same_parity(t, -9))
                dve.tensor_copy(slot_idx[par][:], slot_f[:]).then_inc(slots_known, 1)

            def body(t):
                for k in range(8):
                    if k == 2 and t.odd and t.pair(3):
                        wait(dve, bn_ready, 4 * t.pair(3)[0] + 4)
                    if k == 6 and t.odd and t.pair(-5):
                        wait(dve, bn2_ready, 4 * t.pair(-5)[0] + 4)
                    reduce_unit(t, k)
                    if k == 2 and t.odd and t.pair(-9):
                        place(*t.pair(-9), t)
                    if k == 5 and t.odd and t.pair(-5):
                        normalise_tokens(t.pair(-5)[0])
                    if k == 6 and t.odd and t.pair(-5):
                        aggregate_tokens(t.pair(-5)[0])
                    if k == 5 and not t.odd and t.pair(-6):
                        n, par = t.pair(-6)
                        wait(dve, rstd2_ready, n + 1)
                        if not (t.fixed and n < 2):
                            dve.wait_ge(scattered[par][0], 64 * same_parity(t, -6))
                        for c in range(4):
                            last = dve.tensor_scalar(y_row[par][0][:, c, 0:D], tile_of(n, c), mv2[:, c, 0:1],
                                                     rstd2[:, c:c + 1], ALU.subtract, ALU.mult)
                        last.then_inc(y_ready, 1)
                    if k == 2 and not t.odd and t.pair(-8):
                        choose(*t.pair(-8))
                    if k == 0 and not t.odd and t.pair(2):
                        n, par = t.pair(2)
                        wait(dve, rstd_ready, n + 1)
                        wait(dve, zT_ready, n)
                        for c in range(4):
                            last = dve.tensor_scalar(z[:, c, :], X1[:, bass.ds(n * 4 + c, 1), :].rearrange("p o d -> p (o d)"),
                                                     mv[:, c, 0:1], rstd[:, c:c + 1], ALU.subtract, ALU.mult)
                        last.then_inc(z_ready, 1)
                    if k == 1 and t.odd and t.pair(3):
                        n, par = t.pair(3)
                        dve.wait_ge(x_loaded[par], 16 * (t.i + (t.r + 3) // 4 + 1))
                        wait(dve, z_ready, n)
                        for c in range(4):
                            dve.bn_stats(bn[:, c, :], X1[:, bass.ds(n * 4 + c, 1), :].rearrange("p o d -> p (o d)")).then_inc(bn_ready, 1)
                    if k == 2 and t.odd and t.pair(3):
                        n, par = t.pair(3)
                        for c in range(4):
                            last = dve.bn_aggr(mv[:, c, :], bn[:, c, :])
                        last.then_inc(mv_ready, 1)
                        wait(dve, mv_ready, n + 1)
                        dve.tensor_scalar(var_e[:], mv[:, :, 1], 1.0 + EPS, EPS * EPS, ALU.mult, ALU.add).then_inc(var_ready, 1)
                    if k == 3 and t.batch(3):
                        b, bi, slot = t.batch(3)
                        par = slot % 2
                        wait(dve, av_done, 2 * b + 2)
                        wait(dve, x1_ready, b - 1)
                        dve.transpose(att[par][:].rearrange("p g m d -> p (g m) d"),
                                      ps_av[:].rearrange("p g (u m) -> p g m u", m=8)).then_inc(att_ready, 1)
                    if k == 4 and t.batch(3):
                        wait(dve, att_ready, b + 1)
                        dve.reciprocal(rden[par][:], att[par][:, :, :, DK]).then_inc(rden_ready, 1)
                    if k == 4 and not t.odd and t.pair(2):
                        n, par = t.pair(2)
                        split(n, par, q_proj, q_hi, q_lo, q_lo_ready, q_hi_ready, bq_c)
                    if k == 7 and not t.odd and t.pair(2):
                        n, par = t.pair(2)
                        split(n, par, k_proj, k_hi, k_lo, k_lo_ready, k_hi_ready, bk_c)
                    if k == 4 and t.odd and t.pair(-1):
                        n, par = t.pair(-1)
                        wait(dve, v_proj, n + 1)
                        wait(dve, av_done, 4 * n - 4)
                        dve.tensor_tensor(v_aug[par][:, :, :, 0:DK],
                                          ps_misc[:].rearrange("p (c h d) -> p c h d", c=4, h=H),
                                          bv_s[:].rearrange("p (o h d) -> p o h d", o=1, h=H).to_broadcast([P, 4, H, DK]),
                                          ALU.add).then_inc(v_ready, 1)

            periods(dve, body)
            made = [0]

            def make(ins):
                made[0] += 1
                ins.then_inc(tabling, 1)
                dve.wait_ge(tabling, made[0])

            def over_tiles(a):
                return a[:].unsqueeze(1).to_broadcast([P, FFN_TILES, E])

            dve.wait_ge(filled, B // 2)
            make(dve.tensor_tensor(total[:], fill[:], region[:], ALU.subtract))
            make(dve.tensor_scalar(tiles_i[:, 0, :], total[:], float(SLOTS - 1), None, ALU.add))
            make(dve.tensor_scalar(tiles_i[:, 1, :], tiles_i[:, 0, :], SLOTS.bit_length() - 1, None, ALU.arith_shift_right))
            make(dve.tensor_copy(tiles_f[:], tiles_i[:, 1, :]))
            make(dve.tensor_tensor_scan(tiles_end[:], ones_e[:], tiles_f[:], 0.0, ALU.mult, ALU.add))
            make(dve.tensor_tensor(passed[:], over_tiles(tiles_end),
                                   tile_n[:].unsqueeze(2).to_broadcast([P, FFN_TILES, E]), ALU.is_le))
            make(dve.tensor_reduce(tile_e[:], passed[:], AX.X, ALU.add))
            make(dve.tensor_tensor(passed_end[:], passed[:], over_tiles(tiles_end), ALU.mult))
            make(dve.tensor_reduce(tile_start[:], passed_end[:], AX.X, ALU.max))
            make(dve.tensor_tensor(tile_k[:], tile_n[:], tile_start[:], ALU.subtract))
            make(dve.tensor_scalar(tile_start[:], tile_e[:], float(REGION), None, ALU.mult))
            make(dve.scalar_tensor_tensor(out=tile_row[:], in0=tile_k[:], scalar=float(SLOTS), in1=tile_start[:],
                                          op0=ALU.mult, op1=ALU.add))
            make(dve.tensor_scalar(table[:, :, 0], tile_row[:], float(E * REGION), None, ALU.min))
            make(dve.tensor_scalar(table[:, :, 1], tile_e[:], float(E - 1), None, ALU.min))
            dve.tensor_copy(pad_start[:], fill[:]).then_inc(table_ready, 1)
            dve.wait_ge(table_ready, 1)

            def lo_part(lo, x, hi, s):
                dve.tensor_tensor(lo, x, hi.bitcast(F32), ALU.subtract).then_inc(s, 1)

            def hi_part(hi, x, loaded, value, s):
                dve.wait_ge(loaded, value)
                dve.tensor_copy(hi, x).then_inc(s, 1)

            def body_b(t):
                if t.tile(-2):
                    n, i, r = t.tile(-2)
                    dve.wait_ge(o_psum, n + 1)
                    if since(n, 2):
                        dve.wait_ge(o_tok_psum, n - 1)
                    dve.tensor_scalar(oT[r % 2], ps_o[r % 2], b_cur[r][:, FC:FC + 1], None, ALU.add).then_inc(oT_ready, 1)
                for f in range(FC):
                    if t.tile(0):
                        n, i, r = t.tile(0)
                        dve.wait_ge(h_hi_ready, 4 * n + f + 1)
                        lo_part(h_lo[r % 2][f], h_f32[f % 2], h_hi[r % 2][f], h_lo_ready)
                    if f == 0 and t.tile(0):
                        n, i, r = t.tile(0)
                        hi_part(w2_hi[r % 2], w2_raw[r % 2], w2_loaded[r % 2], loads(i, r, 2), w2_hi_ready)
                    if f == 1 and t.tile(1):
                        n, i, r = t.tile(1)
                        if since(n, 4):
                            dve.wait_ge(added[r % 2], 64 * (i * 2 + r // 2 - 1))
                        dve.wait_ge(y_loaded[r], loads(i, r, 4))
                        dve.tensor_copy(gate_row[r][:, :, 0], y_tile[r][:, :, D])
                        dve.tensor_copy(gate_row[r][:, :, 1].bitcast(I32), y_tile[r][:, :, D + 1].bitcast(I32)).then_inc(gate_row_ready, 1)
                        hi_part(w1_hi[r % 2], w1_raw[r % 2], w1_loaded[r % 2], loads(i, r, 2), w1_hi_ready)
                    if f == 1 and t.tile(-2):
                        n, i, r = t.tile(-2)
                        dve.wait_ge(o_tok_psum, n + 1)
                        if since(n, 2):
                            dve.wait_ge(added[r % 2], 64 * (i * 2 + r // 2))
                        dve.tensor_tensor(res[r % 2].rearrange("p (c d) -> p c d", d=D),
                                          ps_t.rearrange("p (c d) -> p c d", d=D),
                                          gate_row[r][:, :, 0:1].to_broadcast([P, SLOTS // P, D]),
                                          ALU.mult).then_inc(res_ready, 1)
                    if f == 2 and t.tile(1):
                        n, i, r = t.tile(1)
                        dve.wait_ge(w1_hi_ready, n + 1)
                        lo_part(w1_lo[r % 2], w1_raw[r % 2], w1_hi[r % 2], w1_lo_ready)
                    if f == 2 and t.tile(1):
                        n, i, r = t.tile(1)
                        dve.wait_ge(y_hi_ready, n + 1)
                        lo_part(y_lo[r % 2], ps_y, y_hi[r % 2], y_lo_ready)

            steps(dve, body_b)


_INS = ['L0_attn_x', 'L0_attn_Wq', 'L0_attn_bq', 'L0_attn_Wk', 'L0_attn_bk', 'L0_attn_Wv', 'L0_attn_bv', 'L0_attn_gamma', 'L0_attn_beta',
        'L0_ffn_centroids', 'L0_ffn_W1', 'L0_ffn_b1', 'L0_ffn_W2', 'L0_ffn_b2']


def kernel(**inputs):
    import numpy as _np
    import concourse.bacc as _bacc
    from concourse import mybir as _mybir
    from concourse.bass_utils import run_bass_kernel_spmd as _run

    nc = _bacc.Bacc("TRN2", target_bir_lowering=False, num_devices=1)
    arrays, args = {}, []
    for name in _INS:
        a = _np.ascontiguousarray(inputs[name])
        arrays[f"in_{name}_dram"] = a
        args.append(nc.dram_tensor(f"in_{name}_dram", a.shape, _mybir.dt.from_np(a.dtype), kind="ExternalInput").ap())
    args.append(nc.dram_tensor("out_0_dram", (B, S, D), F32, kind="ExternalOutput").ap())
    build(nc, *args)
    r = _run(nc, [arrays], core_ids=[0])
    return r.results[0]["out_0_dram"]
```

```python
from contextlib import ExitStack

import concourse.bass as bass
from concourse import mybir

ALU = mybir.AluOpType
ACT = mybir.ActivationFunctionType
AX = mybir.AxisListType
F32 = mybir.dt.float32
F32R = mybir.dt.float32r
BF16 = mybir.dt.bfloat16
I32 = mybir.dt.int32
U32 = mybir.dt.uint32

P = 128
B, S, D = 32, 256, 128
H = 8
DK = D // H
EPS = 1e-5
TILES = B * S // P
PAIR = 2
RING = 4
M_ROW = 96

E = 8
DFF = 4 * D
FC = DFF // P
TOP_K = 2
SLOTS = 512
ROWS = B * S
REGION = ROWS + SLOTS
FFN_TILES = (ROWS * TOP_K + E * (SLOTS - 1)) // SLOTS
WIDTH = D + 2


def build(nc, x_in, Wq, bq, Wk, bk, Wv, bv, gamma, beta, cent, W1, b1, W2, b2, out):
    with ExitStack() as ctx:
        def sb(name, shape, dt=F32):
            return ctx.enter_context(nc.sbuf_tensor(name, shape, dt))

        def sem(name):
            return ctx.enter_context(nc.semaphore(name))

        X1 = sb("X1", [P, TILES, D])
        q_stack = [sb(f"q_stack{n}", [P, H, S], F32R) for n in range(RING)]
        k_stack = [sb(f"k_stack{n}", [P, H, S], F32R) for n in range(RING)]
        probs = [sb(f"probs{n}", [P, H, 2, S]) for n in range(2)]
        v_aug = [sb(f"v_aug{n}", [P, 4, H, 32]) for n in range(2)]
        q_hi = [sb(f"q_hi{n}", [P, 512], F32R) for n in range(2)]
        q_lo = [sb(f"q_lo{n}", [P, 512], F32R) for n in range(2)]
        k_hi = [sb(f"k_hi{n}", [P, 512], F32R) for n in range(2)]
        k_lo = [sb(f"k_lo{n}", [P, 512], F32R) for n in range(2)]
        xnT = [sb(f"xnT{n}", [P, 512]) for n in range(2)]
        z = sb("z", [P, 4, D])
        row_max = [sb(f"row_max{n}", [P, 2, H]) for n in range(2)]
        neg_maxT = [sb(f"neg_maxT{n}", [H, S], F32R) for n in range(2)]
        att = [sb(f"att{n}", [P, 2, 8, 32]) for n in range(2)]
        rden = [sb(f"rden{n}", [P, 2, 8]) for n in range(2)]
        att_n = [sb(f"att_n{n}", [P, 2, 8, DK]) for n in range(2)]
        bn = sb("bn", [P, 4, 6])
        mv = sb("mv", [P, 4, 2])
        var_e = sb("var_e", [P, 4])
        rstd = sb("rstd", [P, 4])
        minus_half = sb("minus_half", [P, 4])
        ident = sb("ident", [P, P])
        Wq_raw = sb("Wq_raw", [P, D])
        Wk_raw = sb("Wk_raw", [P, D])
        Wq_p = sb("Wq_p", [P, D])
        Wk_p = sb("Wk_p", [P, D])
        Wv_raw = sb("Wv_raw", [P, D * H])
        Wv_s = sb("Wv_s", [P, D])
        bv_raw = sb("bv_raw", [P, D * H])
        bv_s = sb("bv_s", [P, D])
        bq_c = sb("bq_c", [P, 1])
        bk_c = sb("bk_c", [P, 1])
        gamma_c = sb("gamma_c", [P, 1])
        beta_c = sb("beta_c", [P, 1])

        bn2 = sb("bn2", [P, 4, 6])
        mv2 = sb("mv2", [P, 4, 2])
        var2 = sb("var2", [P, 4])
        rstd2 = sb("rstd2", [P, 4])
        y_row = [[sb(f"y_row{n}_{k}", [P, 4, WIDTH]) for k in range(TOP_K)] for n in range(2)]
        yT = sb("yT", [P, 512])
        cent_raw = sb("cent_raw", [E, D])
        centT = sb("centT", [P, E])
        expn = sb("expn", [P, 4, E])
        den = sb("den", [P, 4, E])
        sig = sb("sig", [P, 4, E])
        top = sb("top", [P, 4, 8])
        top_e = sb("top_e", [P, 4, 8], U32)
        top_f = sb("top_f", [P, 4, TOP_K])
        chosen = [sb(f"chosen{k}", [P, 4, E]) for k in range(TOP_K)]
        gate_sum = sb("gate_sum", [P, 4])
        gate_rcp = sb("gate_rcp", [P, 4])
        picked = sb("picked", [P, 5, E], BF16)
        before = sb("before", [P, P], BF16)
        ones_bf = sb("ones_bf", [P, P], BF16)
        fill = sb("fill", [P, E])
        slot_all = sb("slot_all", [P, 4, E])
        slot_sel = [sb(f"slot_sel{k}", [P, 4, E]) for k in range(TOP_K)]
        slot_f = sb("slot_f", [P, TOP_K, 4])
        slot_idx = [sb(f"slot_idx{n}", [P, TOP_K, 4], I32) for n in range(2)]
        expert_i = sb("expert_i", [P, E], I32)
        expert_n = sb("expert_n", [P, E])
        region_i = sb("region_i", [P, E], I32)
        region = sb("region", [P, E])
        token_i = sb("token_i", [P, 4], I32)
        token = sb("token", [P, 4])
        total = sb("total", [P, E])
        tiles_i = sb("tiles_i", [P, 2, E], I32)
        tiles_f = sb("tiles_f", [P, E])
        tiles_end = sb("tiles_end", [P, E])
        ones_e = sb("ones_e", [P, E])
        tile_i = sb("tile_i", [P, FFN_TILES], I32)
        tile_n = sb("tile_n", [P, FFN_TILES])
        passed = sb("passed", [P, FFN_TILES, E])
        passed_end = sb("passed_end", [P, FFN_TILES, E])
        tile_e = sb("tile_e", [P, FFN_TILES])
        tile_start = sb("tile_start", [P, FFN_TILES])
        tile_k = sb("tile_k", [P, FFN_TILES])
        tile_row = sb("tile_row", [P, FFN_TILES])
        table = sb("table", [P, FFN_TILES, 2], I32)
        pad_start = sb("pad_start", [P, E], I32)
        pad_rows = sb("pad_rows", [P, SLOTS // P, WIDTH])
        slots = nc.dram_tensor("slots", (E * REGION + SLOTS, WIDTH), F32).ap()

        b_all = sb("b_all", [P, E, FC + 1])
        b_cur = [sb(f"b_cur{n}", [P, FC + 1]) for n in range(4)]
        tick = [sb(f"tick{n}", [P, 1]) for n in range(2)]
        gate_row = [sb(f"gate_row{n}", [P, SLOTS // P, 2]) for n in range(4)]
        y_tile = [sb(f"y_tile{n}", [P, SLOTS // P, WIDTH]) for n in range(4)]

        ps_max = [ctx.enter_context(nc.psum_tensor(f"ps_max{n}", [P, 2, S], F32)) for n in range(2)]
        ps_st = [ctx.enter_context(nc.psum_tensor(f"ps_st{n}", [P, 2, S], F32)) for n in range(2)]
        ps_av = ctx.enter_context(nc.psum_tensor("ps_av", [P, 2, S], F32))
        ps_proj = ctx.enter_context(nc.psum_tensor("ps_proj", [P, 512], F32))
        ps_mv = ctx.enter_context(nc.psum_tensor("ps_mv", [P, 512], F32))
        ps_route = ctx.enter_context(nc.psum_tensor("ps_route", [P, 512], F32))

        w_loaded = sem("w_loaded")
        w_ready = sem("w_ready")
        const_ready = sem("const_ready")
        zeros_ready = sem("zeros_ready")
        kzeros_ready = sem("kzeros_ready")
        ones_ready = sem("ones_ready")
        x_loaded = [sem(f"x_loaded{n}") for n in range(2)]
        bn_ready = sem("bn_ready")
        mv_ready = sem("mv_ready")
        var_ready = sem("var_ready")
        rstd_ready = sem("rstd_ready")
        z_ready = sem("z_ready")
        zT_ready = sem("zT_ready")
        xnT_ready = sem("xnT_ready")
        q_proj, k_proj, v_proj = sem("q_proj"), sem("k_proj"), sem("v_proj")
        q_hi_ready, q_lo_ready = sem("q_hi_ready"), sem("q_lo_ready")
        k_hi_ready, k_lo_ready = sem("k_hi_ready"), sem("k_lo_ready")
        v_ready = sem("v_ready")
        stack_placed = [sem(f"stack_placed{n}") for n in range(RING)]
        m_placed = [sem(f"m_placed{n}") for n in range(RING)]
        smax_ready = sem("smax_ready")
        smax_reduced = sem("smax_reduced")
        maxT_ready = sem("maxT_ready")
        neg_maxT_ready = sem("neg_maxT_ready")
        st_ready = sem("st_ready")
        exp_done = sem("exp_done")
        av_done = sem("av_done")
        att_ready = sem("att_ready")
        rden_ready = sem("rden_ready")
        att_n_ready = sem("att_n_ready")
        x1_ready = sem("x1_ready")
        stored = sem("stored")

        x1_stored = sem("x1_stored")
        b_loaded = sem("b_loaded")
        tabling, table_ready = sem("tabling"), sem("table_ready")
        padded = sem("padded")
        y_loaded = [sem(f"y_loaded{n}") for n in range(4)]
        w1_loaded = [sem(f"w1_loaded{n}") for n in range(2)]
        w2_loaded = [sem(f"w2_loaded{n}") for n in range(2)]
        w1_hi_ready, w1_lo_ready = sem("w1_hi_ready"), sem("w1_lo_ready")
        w2_hi_ready, w2_lo_ready = sem("w2_hi_ready"), sem("w2_lo_ready")
        b_ready = sem("b_ready")
        yT2_psum, y_hi_ready, y_lo_ready = sem("yT2_psum"), sem("y_hi_ready"), sem("y_lo_ready")
        h_psum, h_f32_ready, h_hi_ready, h_lo_ready = sem("h_psum"), sem("h_f32_ready"), sem("h_hi_ready"), sem("h_lo_ready")
        o_psum, oT_ready, o_tok_psum, res_ready = sem("o_psum"), sem("oT_ready"), sem("o_tok_psum"), sem("res_ready")
        added = [sem(f"added{n}") for n in range(2)]
        ticked = sem("ticked")
        gate_row_ready = sem("gate_row_ready")
        cent_loaded = sem("cent_loaded")
        centT_psum, centT_ready = sem("centT_psum"), sem("centT_ready")
        iota_ready = sem("iota_ready")
        floats_ready = sem("floats_ready")
        route_const = sem("route_const")
        bn2_ready, mv2_ready = sem("bn2_ready"), sem("mv2_ready")
        var2_ready, rstd2_ready = sem("var2_ready"), sem("rstd2_ready")
        y_ready, y_copied = sem("y_ready"), sem("y_copied")
        yT_psum, yT_ready = sem("yT_psum"), sem("yT_ready")
        logits_ready, expn_ready = sem("logits_ready"), sem("expn_ready")
        gating = sem("gating")
        picked_ready = sem("picked_ready")
        rank_ready = sem("rank_ready")
        filled, slots_known = sem("filled"), sem("slots_known")
        scattered = [[sem(f"scattered{n}_{k}") for k in range(TOP_K)] for n in range(2)]

        N_W = 8 * 16
        GATING = 13

        def wait(eng, s, value):
            if not isinstance(value, int) or value > 0:
                eng.wait_ge(s, value)

        class Period:

            def __init__(self, i, r):
                self.i, self.r, self.fixed = i, r, isinstance(i, int)
                self.odd = r % 2 == 1

            def batch(self, lag):
                o = self.r - lag
                b = self.i * 4 + o
                if self.fixed and not 0 <= b < B:
                    return None
                return b, self.i + o // 4, o % 4

            def pair(self, lead):
                o = self.r + lead
                assert o % 2 == 0
                n = self.i * 2 + o // 2
                if self.fixed and not 0 <= n < B // 2:
                    return None
                return n, (o // 2) % 2

        def same_parity(t, lead):
            return t.i + (t.r + lead) // 4

        def periods(eng, body):
            for j in range(-4, 12):
                body(Period(j // 4, j % 4))
            with eng.Fori(3, 7) as i:
                for r in range(4):
                    body(Period(i, r))
            for j in range(28, 42):
                body(Period(j // 4, j % 4))

        def cols(t, first, count):
            pattern = "p h t s -> p (h t s)" if len(t.shape) == 4 else "p h s -> p (h s)"
            return t[:].rearrange(pattern)[:, first * 512:(first + count) * 512]

        w1_raw = [cols(probs[0], n, 1) for n in range(2)]
        w2_raw = [cols(probs[0], 2 + n, 1) for n in range(2)]
        h_f32 = [cols(probs[1], n, 1) for n in range(2)]
        oT = [cols(probs[1], 2 + n, 1) for n in range(2)]
        res = [cols(probs[1], 4 + n, 1) for n in range(2)]
        w1_hi = [cols(q_stack[0], n, 1) for n in range(2)]
        w2_hi = [cols(q_stack[0], 2 + n, 1) for n in range(2)]
        w1_lo = [cols(q_stack[1], n, 1) for n in range(2)]
        w2_lo = [cols(q_stack[1], 2 + n, 1) for n in range(2)]
        y_hi = [cols(q_stack[2], n, 1) for n in range(2)]
        y_lo = [cols(q_stack[2], 2 + n, 1) for n in range(2)]
        h_hi = [[cols(k_stack[n], f, 1) for f in range(FC)] for n in range(2)]
        h_lo = [[cols(k_stack[2 + n], f, 1) for f in range(FC)] for n in range(2)]
        ps_h = [ps_st[n][:].rearrange("p a s -> p (a s)") for n in range(2)] + [ps_proj[:], ps_mv[:]]
        ps_o = [ps_max[n][:].rearrange("p a s -> p (a s)") for n in range(2)]
        ps_y = ps_av[:].rearrange("p a s -> p (a s)")
        ps_t = ps_route[:]

        class Step:

            def __init__(self, i, r):
                self.i, self.r, self.fixed = i, r, isinstance(i, int)

            def tile(self, lead):
                o = self.r + lead
                n = self.i * 4 + o
                if self.fixed and not 0 <= n < FFN_TILES:
                    return None
                return n, self.i + o // 4, o % 4

        def steps(eng, body):
            last = (FFN_TILES - 3) // 4
            for t in range(-2, 4):
                body(Step(t // 4, t % 4))
            with eng.Fori(1, last) as i:
                for r in range(4):
                    body(Step(i, r))
            for t in range(4 * last, FFN_TILES + 2):
                body(Step(t // 4, t % 4))

        def since(n, back):
            return not isinstance(n, int) or n >= back

        def loads(i, r, ring):
            return 16 * (i + 1) if ring == 4 else 16 * (i * 2 + r // 2 + 1)

        block = ctx.enter_context(nc.Block())

        @block.sync
        def _(sp):
            xt = x_in.rearrange("b (c p) d -> p (b c) d", p=P)
            out_t = out.rearrange("b (c p) d -> p (b c) d", p=P)

            def load_x(n, par):
                sp.dma_start(X1[:, bass.ds(n * 4, 4), :], xt[:, bass.ds(n * 4, 4), :]).then_inc(x_loaded[par], 16)

            load_x(0, 0)
            sp.dma_start(gamma_c[:], gamma.rearrange("(p o) -> p o", o=1)).then_inc(w_loaded, 16)
            sp.dma_start(beta_c[:], beta.rearrange("(p o) -> p o", o=1)).then_inc(w_loaded, 16)
            sp.dma_start(Wq_raw[:], Wq).then_inc(w_loaded, 16)
            sp.dma_start(Wk_raw[:], Wk).then_inc(w_loaded, 16)
            sp.dma_start(bq_c[:], bq.rearrange("(h d o) -> d h o", h=H, o=1), allow_slow_non_contiguous=True).then_inc(w_loaded, 16)
            sp.dma_start(bk_c[:], bk.rearrange("(h d o) -> d h o", h=H, o=1), allow_slow_non_contiguous=True).then_inc(w_loaded, 16)
            sp.dma_start(Wv_raw[:], Wv).then_inc(w_loaded, 16)
            sp.dma_start(bv_raw[:], bv.rearrange("(o n) -> o n", o=1).broadcast_to([P, D * H])).then_inc(w_loaded, 16)
            load_x(1, 1)

            def body(t):
                if not t.odd:
                    p = t.pair(4)
                    if p and not (t.fixed and p[0] < 2):
                        wait(sp, bn_ready, 4 * (p[0] - 1))
                        load_x(*p)
                nb = t.batch(-1)
                if nb:
                    b, bi, slot = nb
                    n = bi * 2 + slot // 2
                    par = (slot // 2) % 2
                    wait(sp, q_lo_ready, n + 1)
                    wait(sp, k_lo_ready, n + 1)
                    wait(sp, st_ready, 8 * b - 24)
                    half = slice((slot % 2) * S, (slot % 2) * S + S)
                    for part, (qs, ks) in enumerate(((q_hi, k_hi), (q_lo, k_hi), (q_hi, k_lo))):
                        for stack, src in ((q_stack, qs), (k_stack, ks)):
                            sp.dma_start(
                                stack[slot][part * DK:(part + 1) * DK, :, :].rearrange("p h s -> p (h s)").bitcast(F32),
                                src[par][:, half].bitcast(F32)).then_inc(stack_placed[slot], 16)
                nb = t.batch(4)
                if nb:
                    b = nb[0]
                    wait(sp, x1_ready, b + 1)
                    sp.dma_start(out_t[:, bass.ds(b * 2, 2), :], X1[:, bass.ds(b * 2, 2), :]).then_inc(x1_stored, 16)

            sp.dma_start(cent_raw[:], cent).then_inc(cent_loaded, 16)
            for f in range(FC):
                sp.dma_start(b_all[:, :, f:f + 1], b1.rearrange("e (f p o) -> f p e o", p=P, o=1)[f],
                             allow_slow_non_contiguous=True).then_inc(b_loaded, 16)
            sp.dma_start(b_all[:, :, FC:FC + 1], b2.rearrange("e (p o) -> p e o", o=1),
                         allow_slow_non_contiguous=True).then_inc(b_loaded, 16)
            sp.wait_ge(zeros_ready, 1)
            sp.wait_ge(kzeros_ready, 1)
            periods(sp, body)
            for n in range(2):
                for k in range(TOP_K):
                    sp.wait_ge(scattered[n][k], 64 * B // 4)
            sp.wait_ge(table_ready, 1)
            tiled = slots.rearrange("(c p) w -> p c w", p=P)
            sp.dma_start(tiled[:, E * REGION // P:, :], pad_rows[:]).then_inc(padded, 16)
            for e in range(E):
                start = sp.value_load(pad_start[0:1, e:e + 1], min_val=e * REGION, max_val=e * REGION + ROWS)
                sp.dma_start(slots[bass.ds(start, SLOTS), :].rearrange("(c p) w -> p c w", p=P),
                             pad_rows[:]).then_inc(padded, 16)

            def load(t):
                if t.tile(2):
                    n, i, r = t.tile(2)
                    e = sp.value_load(table[0:1, bass.ds(n, 1), 1:2].rearrange("p a b -> p (a b)"), min_val=0, max_val=E - 1)
                    row = sp.value_load(table[0:1, bass.ds(n, 1), 0:1].rearrange("p a b -> p (a b)"), min_val=0, max_val=E * REGION)
                    if not since(n, 1):
                        sp.wait_ge(padded, 16 * (E + 1))
                    if since(n, 4):
                        sp.wait_ge(yT2_psum, n - 3)
                        sp.wait_ge(gate_row_ready, n - 3)
                    sp.dma_start(y_tile[r][:], slots[bass.ds(row, SLOTS), :].rearrange("(c p) w -> p c w", p=P)).then_inc(y_loaded[r], 16)
                    if since(n, 2):
                        sp.wait_ge(w1_lo_ready, n - 1)
                    sp.dma_start(w1_raw[r % 2], W1[bass.ds(e, 1), :, :].rearrange("e d f -> d (e f)")).then_inc(w1_loaded[r % 2], 16)
                if t.tile(1):
                    n, i, r = t.tile(1)
                    e = sp.value_load(table[0:1, bass.ds(n, 1), 1:2].rearrange("p a b -> p (a b)"), min_val=0, max_val=E - 1)
                    if since(n, 2):
                        sp.wait_ge(w2_lo_ready, n - 1)
                    sp.dma_start(w2_raw[r % 2].rearrange("p (f d) -> p f d", f=FC),
                                 W2[bass.ds(e, 1), :, :].rearrange("e (f p) d -> p (e f) d", p=P)).then_inc(w2_loaded[r % 2], 16)

            steps(sp, load)

        @block.gpsimd
        def _(pool):
            pool.memset(minus_half[:], -0.5).then_inc(const_ready, 1)
            pool.memset(ident[:], 0.0).then_inc(const_ready, 1)
            for n in range(RING):
                pool.memset(k_stack[n][:].bitcast(F32), 0.0)
            for n in range(2):
                last = pool.memset(v_aug[n][:], 0.0)
            last.then_inc(kzeros_ready, 1)
            pool.wait_ge(kzeros_ready, 1)
            for n in range(RING):
                last = pool.memset(k_stack[n][M_ROW:M_ROW + 1, :, :].bitcast(F32), 1.0)
            last.then_inc(kzeros_ready, 1)
            pool.wait_ge(kzeros_ready, 2)
            for n in range(2):
                last = pool.memset(v_aug[n][:, :, :, DK:DK + 1], 1.0)
            last.then_inc(ones_ready, 1)
            pool.iota(expert_i[:], pattern=[[1, E]], base=0, channel_multiplier=0).then_inc(iota_ready, 1)
            pool.iota(region_i[:], pattern=[[REGION, E]], base=0, channel_multiplier=0).then_inc(iota_ready, 1)
            pool.iota(token_i[:], pattern=[[P, 4]], base=0, channel_multiplier=1).then_inc(iota_ready, 1)
            pool.iota(tile_i[:], pattern=[[1, FFN_TILES]], base=0, channel_multiplier=0).then_inc(iota_ready, 1)
            pool.memset(ones_bf[:], 1.0).then_inc(route_const, 1)
            pool.memset(ones_e[:], 1.0).then_inc(route_const, 1)
            pool.memset(picked[:], 0.0).then_inc(route_const, 1)
            pool.memset(pad_rows[:], 0.0).then_inc(route_const, 1)
            pool.memset(tick[0][:], 0.0).then_inc(route_const, 1)
            pool.wait_ge(route_const, 5)
            pool.affine_select(out=before[:], in_=ones_bf[:], compare_op=ALU.is_gt, fill=0.0, base=0,
                               pattern=[[1, P]], channel_multiplier=-1).then_inc(route_const, 1)
            pool.memset(pad_rows[:, :, D + 1].bitcast(I32), 2 * ROWS).then_inc(route_const, 1)
            pool.wait_ge(const_ready, 2)
            pool.affine_select(out=ident[:], in_=ident[:], compare_op=ALU.not_equal, fill=1.0, base=0,
                               pattern=[[-1, P]], channel_multiplier=1).then_inc(const_ready, 1)

            def body(t):
                nb = t.batch(3)
                if nb:
                    b, bi, slot = nb
                    par = slot % 2
                    wait(pool, rden_ready, b + 1)
                    pool.tensor_tensor(att_n[par][:], att[par][:, :, :, 0:DK],
                                       rden[par][:].unsqueeze(3).to_broadcast([P, 2, 8, DK]),
                                       ALU.mult).then_inc(att_n_ready, 1)
                    wait(pool, att_n_ready, b + 1)
                    xs = X1[:, bass.ds(b * 2, 2), :]
                    pool.tensor_tensor(xs, xs, att_n[par][:].rearrange("p g m d -> p g (m d)"),
                                       ALU.add).then_inc(x1_ready, 1)
                src, dst, ready, used, done, pn = ((var2, rstd2, var2_ready, y_ready, rstd2_ready, t.pair(-5)) if t.odd else
                                                   (var_e, rstd, var_ready, z_ready, rstd_ready, t.pair(4)))
                k, pr = (0, t.pair(-9)) if t.odd else (1, t.pair(-10))
                if pr:
                    wait(pool, slots_known, pr[0] + 1)
                if pn:
                    wait(pool, ready, pn[0] + 1)
                    wait(pool, used, pn[0])
                    pool.tensor_tensor(dst[:], src[:], minus_half[:], ALU.pow).then_inc(done, 1)
                if pr:
                    n, par_s = pr
                    for c in range(4):
                        pool.indirect_dma_start(slots, bass.IndirectOffsetOnAxis(slot_idx[par_s][:, k, c:c + 1], 0),
                                                y_row[par_s][k][:, c, :], None).then_inc(scattered[par_s][k], 16)

            periods(pool, body)
            out_rows = out.rearrange("b s d -> (b s) d")
            pool.wait_ge(table_ready, 1)

            pool.wait_ge(x1_stored, 16 * B)
            last_row = pool.to_reg(ROWS - 1)

            def expert(t):
                if t.tile(1):
                    n, i, r = t.tile(1)
                    e = pool.value_load(table[0:1, bass.ds(n, 1), 1:2].rearrange("p a b -> p (a b)"), min_val=0, max_val=E - 1)
                    if since(n, 4):
                        pool.wait_ge(oT_ready, n - 3)
                    pool.wait_ge(b_loaded, 16 * (FC + 1))
                    pool.tensor_copy(b_cur[r][:], b_all[:, bass.ds(e, 1), :].rearrange("p a b -> p (a b)")).then_inc(b_ready, 1)
                if t.tile(0):
                    n, i, r = t.tile(0)
                    pool.wait_ge(w2_hi_ready, n + 1)
                    if since(n, 2):
                        pool.wait_ge(o_psum, n - 1)
                    pool.tensor_tensor(w2_lo[r % 2], w2_raw[r % 2], w2_hi[r % 2].bitcast(F32), ALU.subtract).then_inc(w2_lo_ready, 1)
                if t.tile(-2):
                    n, i, r = t.tile(-2)
                    par = r % 2
                    pool.wait_ge(res_ready, n + 1)
                    if since(n, 1):
                        o = r - 1
                        pool.wait_ge(added[o % 2], 64 * ((i + o // 4) * 2 + (o % 4) // 2 + 1))
                    pool.wait_ge(gate_row_ready, n + 1)
                    if since(n, 1):
                        pool.wait_ge(ticked, n)
                    pool.tensor_tensor(tick[1][:], tick[0][:], tick[0][:], ALU.add).then_inc(ticked, 1)
                    for c in range(SLOTS // P):
                        pool.indirect_dma_start(
                            out_rows, bass.IndirectOffsetOnAxis(gate_row[r][:, c, 1:2].bitcast(I32), 0),
                            res[par][:, c * P:(c + 1) * P], None, bounds_check=last_row, oob_is_err=False,
                            compute_op=ALU.add).then_inc(added[par], 16)

            steps(pool, expert)
            pool.wait_ge(added[0], 64 * ((FFN_TILES + 1) // 2))
            pool.wait_ge(added[1], 64 * (FFN_TILES // 2))

        @block.scalar
        def _(act):
            act.wait_ge(w_loaded, N_W)
            act.wait_ge(centT_psum, 1)
            act.activation(centT[:], ps_route[:, 0:E], ACT.Copy).then_inc(centT_ready, 1)
            act.activation(Wq_p[:].rearrange("p (d h) -> p d h", h=H),
                           Wq_raw[:].rearrange("p (h d) -> p d h", h=H), ACT.Copy).then_inc(w_ready, 1)
            act.activation(Wk_p[:].rearrange("p (d h) -> p d h", h=H),
                           Wk_raw[:].rearrange("p (h d) -> p d h", h=H), ACT.Copy).then_inc(w_ready, 1)

            def exps(t, h):
                nb = t.batch(2)
                if nb:
                    b, bi, slot = nb
                    if h == 0:
                        wait(act, av_done, 2 * b - 2)
                    wait(act, st_ready, 8 * b + h + 1)
                    act.activation(probs[slot % 2][:, h, :, :], ps_st[h % 2][:], ACT.Exp,
                                   scale=DK ** -0.5).then_inc(exp_done, 1)

            def body(t):
                prep = t.pair(3) if t.odd else None
                prep_k = None if t.odd else t.pair(2)
                ry = t.pair(-7) if t.odd else None
                rl = None if t.odd else t.pair(-8)
                for h in range(H):
                    exps(t, h)
                    if h == 0 and rl:
                        wait(act, logits_ready, rl[0] + 1)
                        wait(act, gating, GATING * rl[0])
                        act.activation(expn[:], ps_route[:, 0:4 * E].rearrange("p (c e) -> p c e", e=E), ACT.Exp,
                                       scale=-1.0).then_inc(expn_ready, 1)
                    if h == 1 and t.batch(1):
                        b, bi, slot = t.batch(1)
                        wait(act, maxT_ready, b + 1)
                        if not (t.fixed and b < 2):
                            o = slot - 2
                            act.wait_ge(m_placed[o % 4], 16 * (bi + o // 4 + 1))
                        act.activation(neg_maxT[slot % 2][:], ps_mv[0:H, 0:S], ACT.Copy, scale=-1.0).then_inc(neg_maxT_ready, 1)
                    if h == 2 and t.batch(1):
                        b, bi, slot = t.batch(1)
                        wait(act, neg_maxT_ready, b + 1)
                        act.wait_ge(stack_placed[slot], 96 * (bi + 1))
                        act.dma_start(q_stack[slot][M_ROW:M_ROW + 1, :, :].rearrange("p h s -> p (h s)").bitcast(F32),
                                      neg_maxT[slot % 2][:].bitcast(F32)).then_inc(m_placed[slot], 16)
                    if h == 3 and prep_k:
                        n, par = prep_k
                        wait(act, k_proj, n + 1)
                        act.activation(k_hi[par][:], ps_proj[:], ACT.Identity, bias=bk_c[:, 0:1]).then_inc(k_hi_ready, 1)
                    if h == 4 and prep:
                        n, par = prep
                        wait(act, zT_ready, n + 1)
                        wait(act, v_proj, n - 1)
                        act.activation(xnT[par][:], ps_proj[:], ACT.Identity, bias=beta_c[:, 0:1],
                                       scale=gamma_c[:, 0:1]).then_inc(xnT_ready, 1)
                    if h == 6 and prep:
                        n, par = prep
                        wait(act, q_proj, n + 1)
                        if not (t.fixed and n < 2):
                            for o in (t.r + 3 - 4, t.r + 3 - 3):
                                act.wait_ge(stack_placed[o % 4], 96 * (t.i + o // 4 + 1))
                        act.activation(q_hi[par][:], ps_proj[:], ACT.Identity, bias=bq_c[:, 0:1]).then_inc(q_hi_ready, 1)
                    if h == 6 and ry:
                        ny, py = ry
                        wait(act, yT_psum, ny + 1)
                        act.activation(yT[:], ps_route[:], ACT.Copy).then_inc(yT_ready, 1)
                    if h == 7 and ry:
                        wait(act, y_ready, ny + 1)
                        if not (t.fixed and ny < 2):
                            act.wait_ge(scattered[py][1], 64 * same_parity(t, -7))
                        act.activation(y_row[py][1][:, :, 0:D], y_row[py][0][:, :, 0:D], ACT.Copy).then_inc(y_copied, 1)

            periods(act, body)
            act.wait_ge(table_ready, 1)

            def hidden(t, f):
                if t.tile(0):
                    n, i, r = t.tile(0)
                    par = r % 2
                    if f == 0:
                        act.wait_ge(b_ready, n + 1)
                    act.wait_ge(h_psum, 4 * n + f + 1)
                    if not (t.fixed and 4 * n + f < 2):
                        act.wait_ge(h_lo_ready, 4 * n + f - 1)
                    act.activation(h_f32[f % 2], ps_h[f], ACT.Gelu, bias=b_cur[r][:, f:f + 1]).then_inc(h_f32_ready, 1)
                    if f == 0 and since(n, 2):
                        act.wait_ge(o_psum, n - 1)
                    act.activation(h_hi[par][f], ps_h[f], ACT.Gelu, bias=b_cur[r][:, f:f + 1]).then_inc(h_hi_ready, 1)

            def body_b(t):
                hidden(t, 0)
                if t.tile(1):
                    n, i, r = t.tile(1)
                    act.wait_ge(yT2_psum, n + 1)
                    act.activation(y_hi[r % 2], ps_y, ACT.Copy).then_inc(y_hi_ready, 1)
                hidden(t, 1)
                hidden(t, 2)
                hidden(t, 3)

            steps(act, body_b)

        @block.tensor
        def _(pe):
            pe.wait_ge(const_ready, 3)
            pe.wait_ge(cent_loaded, 16)
            pe.transpose(ps_route[:, 0:E], cent_raw[:], ident[0:E, 0:E]).then_inc(centT_psum, 1)
            pe.wait_ge(centT_ready, 1)
            pe.wait_ge(ones_ready, 1)
            pe.wait_ge(w_ready, 4)
            pe.wait_ge(route_const, 7)

            def max_unit(t, k):
                nb = t.batch(0)
                if nb:
                    b, bi, slot = nb
                    if k == 0:
                        pe.wait_ge(stack_placed[slot], 96 * (bi + 1))
                    sc, hp = k // 4, k % 4
                    wait(pe, smax_reduced, 8 * b + k - 1)
                    for hh in range(2):
                        h = 2 * hp + hh
                        last = pe.matmul(ps_max[k % 2][:, hh, :], q_stack[slot][0:M_ROW, h, sc * P:(sc + 1) * P],
                                         k_stack[slot][0:M_ROW, h, :], start=True, stop=True)
                    last.then_inc(smax_ready, 1)

            def st_unit(t, h):
                nb = t.batch(2)
                if nb:
                    b, bi, slot = nb
                    if h == 0:
                        pe.wait_ge(m_placed[slot], 16 * (bi + 1))
                    wait(pe, exp_done, 8 * b + h - 1)
                    for tc in range(2):
                        last = pe.matmul(ps_st[h % 2][:, tc, :], k_stack[slot][:, h, tc * P:(tc + 1) * P],
                                         q_stack[slot][:, h, :], start=True, stop=True)
                    last.then_inc(st_ready, 1)

            def av(t, lag, g):
                nb = t.batch(lag)
                if nb:
                    b, bi, slot = nb
                    n = bi * 2 + slot // 2
                    if g == 0:
                        wait(pe, v_ready, n + 1)
                        wait(pe, att_ready, b)
                    wait(pe, exp_done, 8 * b + 4 * g + 4)
                    for tc in range(2):
                        for j in range(4):
                            h = 4 * g + j
                            last = pe.matmul(ps_av[32 * j:32 * j + 32, g, :],
                                             v_aug[(slot // 2) % 2][:, 2 * (slot % 2) + tc, h, :],
                                             probs[slot % 2][:, h, tc, :], start=(tc == 0), stop=(tc == 1),
                                             tile_position=(0, 32 * j))
                    last.then_inc(av_done, 1)

            def body(t):
                prep = t.pair(3) if t.odd else None
                prep_k = None if t.odd else t.pair(2)
                prep_v = None if t.odd else t.pair(0)
                rank_n = t.pair(-9) if t.odd else None
                route = t.pair(-7) if t.odd else None
                for k in range(8):
                    max_unit(t, k)
                    if k == 1 and t.batch(1):
                        b, bi, slot = t.batch(1)
                        wait(pe, smax_reduced, 8 * b + 8)
                        wait(pe, neg_maxT_ready, b)
                        if t.odd and t.pair(-1):
                            wait(pe, v_ready, t.pair(-1)[0] + 1)
                        for sc in range(2):
                            last = pe.transpose(ps_mv[0:H, sc * P:(sc + 1) * P], row_max[slot % 2][:, sc, :], ident[:])
                        last.then_inc(maxT_ready, 1)
                    if k == 1 and prep_k:
                        n, par = prep_k
                        wait(pe, q_hi_ready, n + 1)
                        wait(pe, q_lo_ready, n + 1)
                        pe.matmul(ps_proj[:], Wk_p[:], xnT[par][:], start=True, stop=True).then_inc(k_proj, 1)
                    if k == 2 and rank_n:
                        wait(pe, picked_ready, rank_n[0] + 1)
                        rank = ps_route[:, 0:5 * E]
                        pe.matmul(rank, before[:], picked[:].rearrange("p c e -> p (c e)"), start=True, stop=False)
                        for c in range(4):
                            last = pe.matmul(rank[:, (c + 1) * E:5 * E], ones_bf[:],
                                             picked[:, c:c + 1, :].to_broadcast([P, 4 - c, E]),
                                             start=False, stop=(c == 3))
                        last.then_inc(rank_ready, 1)
                    if k == 3 and prep:
                        n, par = prep
                        wait(pe, z_ready, n + 1)
                        wait(pe, k_hi_ready, n)
                        wait(pe, k_lo_ready, n)
                        for c in range(4):
                            last = pe.transpose(ps_proj[:, c * P:(c + 1) * P], z[:, c, :], ident[:])
                        last.then_inc(zT_ready, 1)
                    if k == 5 and prep:
                        n, par = prep
                        wait(pe, xnT_ready, n + 1)
                        pe.matmul(ps_proj[:], Wq_p[:], xnT[par][:], start=True, stop=True).then_inc(q_proj, 1)
                    if k == 5 and route:
                        ny, py = route
                        wait(pe, y_ready, ny + 1)
                        if rank_n:
                            wait(pe, filled, rank_n[0] + 1)
                        elif ny > 0:
                            wait(pe, expn_ready, ny)
                        for c in range(4):
                            last = pe.transpose(ps_route[:, c * P:(c + 1) * P], y_row[py][0][:, c, 0:D], ident[:])
                        last.then_inc(yT_psum, 1)
                    if k == 7 and route:
                        wait(pe, yT_ready, ny + 1)
                        for c in range(4):
                            last = pe.matmul(ps_route[:, c * E:(c + 1) * E], yT[:, c * P:(c + 1) * P], centT[:],
                                             start=True, stop=True)
                        last.then_inc(logits_ready, 1)
                    if k == 5 and prep_v:
                        n, par = prep_v
                        if t.batch(1):
                            wait(pe, neg_maxT_ready, t.batch(1)[0] + 1)
                        for c in range(4):
                            last = pe.matmul(ps_mv[:, c * P:(c + 1) * P], xnT[par][:, c * P:(c + 1) * P], Wv_s[:],
                                             start=True, stop=True)
                        last.then_inc(v_proj, 1)
                    st_unit(t, k)
                    if k == 2:
                        av(t, 3, 1)
                    if k == 6:
                        av(t, 2, 0)

            periods(pe, body)
            pe.wait_ge(table_ready, 1)

            def three(o, w_hi, w_lo, x_hi, x_lo, start, stop):
                pe.matmul(o, w_hi, x_hi, start=start, stop=False)
                pe.matmul(o, w_lo, x_hi, start=False, stop=False)
                return pe.matmul(o, w_hi, x_lo, start=False, stop=stop)

            def body_b(t):
                for f in range(FC):
                    part = slice(f * P, (f + 1) * P)
                    if t.tile(0):
                        n, i, r = t.tile(0)
                        par = r % 2
                        if f == 0:
                            pe.wait_ge(w1_hi_ready, n + 1)
                            pe.wait_ge(w1_lo_ready, n + 1)
                            pe.wait_ge(y_lo_ready, n + 1)
                        if since(n, 1):
                            pe.wait_ge(h_hi_ready, 4 * (n - 1) + f + 1)
                        three(ps_h[f], w1_hi[par][:, part], w1_lo[par][:, part], y_hi[par], y_lo[par],
                              True, True).then_inc(h_psum, 1)
                    if t.tile(-1):
                        n, i, r = t.tile(-1)
                        par = r % 2
                        if f == 0:
                            pe.wait_ge(w2_hi_ready, n + 1)
                            pe.wait_ge(w2_lo_ready, n + 1)
                            if since(n, 2):
                                pe.wait_ge(oT_ready, n - 1)
                        pe.wait_ge(h_lo_ready, 4 * n + f + 1)
                        last = three(ps_o[par], w2_hi[par][:, part], w2_lo[par][:, part], h_hi[par][f], h_lo[par][f],
                                     f == 0, f == FC - 1)
                        if f == FC - 1:
                            last.then_inc(o_psum, 1)
                    if f == 1 and t.tile(-2):
                        n, i, r = t.tile(-2)
                        pe.wait_ge(oT_ready, n + 1)
                        if since(n, 1):
                            pe.wait_ge(res_ready, n)
                        for c in range(SLOTS // P):
                            last = pe.transpose(ps_t[:, c * P:(c + 1) * P], oT[r % 2][:, c * P:(c + 1) * P], ident[:])
                        last.then_inc(o_tok_psum, 1)
                    if f == 0 and t.tile(1):
                        n, i, r = t.tile(1)
                        pe.wait_ge(y_loaded[r], loads(i, r, 4))
                        if since(n, 1):
                            pe.wait_ge(y_lo_ready, n)
                        for c in range(SLOTS // P):
                            last = pe.transpose(ps_y[:, c * P:(c + 1) * P], y_tile[r][:, c, 0:D], ident[:])
                        last.then_inc(yT2_psum, 1)

            steps(pe, body_b)

        @block.vector
        def _(dve):
            for n in range(RING):
                last = dve.memset(q_stack[n][:].bitcast(F32), 0.0)
            last.then_inc(zeros_ready, 1)
            dve.wait_ge(iota_ready, 4)
            for dst, src in ((expert_n, expert_i), (region, region_i), (fill, region_i), (token, token_i), (tile_n, tile_i)):
                dve.tensor_copy(dst[:], src[:]).then_inc(floats_ready, 1)
            dve.wait_ge(floats_ready, 5)
            dve.wait_ge(w_loaded, N_W)
            dve.tensor_reduce(Wv_s[:], Wv_raw[:].rearrange("p (n g) -> p n g", g=8), AX.X, ALU.add).then_inc(w_ready, 1)
            dve.tensor_reduce(bv_s[:], bv_raw[:].rearrange("p (n g) -> p n g", g=8), AX.X, ALU.add).then_inc(w_ready, 1)

            def reduce_unit(t, k):
                nb = t.batch(0)
                if nb:
                    b, bi, slot = nb
                    if k == 0:
                        wait(dve, maxT_ready, b - 1)
                    sc, hp = k // 4, k % 4
                    wait(dve, smax_ready, 8 * b + k + 1)
                    dve.tensor_reduce(row_max[slot % 2][:, sc, 2 * hp:2 * hp + 2], ps_max[k % 2][:], AX.X,
                                      ALU.max).then_inc(smax_reduced, 1)

            def split(n, par, src_ready, hi, lo, lo_ready, hi_ready, bias):
                wait(dve, hi_ready, n + 1)
                dve.scalar_tensor_tensor(out=lo[par][:], in0=ps_proj[:], scalar=bias[:, 0:1], in1=hi[par][:].bitcast(F32),
                                         op0=ALU.add, op1=ALU.subtract).then_inc(lo_ready, 1)

            def own(n, count):
                wait(dve, gating, GATING * n + count)

            def step(ins):
                ins.then_inc(gating, 1)

            def over_e(a):
                return a[:].unsqueeze(2).to_broadcast([P, 4, E])

            def tile_of(n, c):
                return X1[:, bass.ds(n * 4 + c, 1), :].rearrange("p o d -> p (o d)")

            def choose(k, n, par):
                if k == 2:
                    wait(dve, expn_ready, n + 1)
                    step(dve.tensor_scalar(den[:], expn[:], 1.0, None, ALU.add))
                if k == 3:
                    own(n, 1)
                    step(dve.reciprocal(sig[:], den[:]))
                if k == 4:
                    for c in range(4):
                        last = dve.max(top[:, c, :], sig[:, c, :])
                    step(last)
                if k == 5:
                    for c in range(4):
                        last = dve.max_index(top_e[:, c, :], top[:, c, :], sig[:, c, :])
                    step(last)
                if k == 6:
                    own(n, 4)
                    step(dve.tensor_copy(top_f[:], top_e[:, :, 0:TOP_K]))
                if k == 7:
                    own(n, 5)
                    for c in range(TOP_K):
                        last = dve.tensor_tensor(chosen[c][:], expert_n[:].unsqueeze(1).to_broadcast([P, 4, E]),
                                                 top_f[:, :, c:c + 1].to_broadcast([P, 4, E]), ALU.is_equal)
                    step(last)

            def place(k, n, par, t):
                rank = ps_route[:, 0:5 * E].rearrange("p (c e) -> p c e", e=E)
                if k == 0:
                    own(n, 6)
                    wait(dve, rank_ready, n)
                    dve.tensor_tensor(picked[:, 0:4, :], chosen[0][:], chosen[1][:], ALU.add).then_inc(picked_ready, 1)
                    step(dve.tensor_tensor(gate_sum[:], top[:, :, 0], top[:, :, 1], ALU.add))
                if k == 2:
                    own(n, 7)
                    step(dve.reciprocal(gate_rcp[:], gate_sum[:]))
                if k == 3:
                    own(n, 8)
                    wait(dve, y_copied, n + 1)
                    for c in range(TOP_K):
                        dve.tensor_tensor(y_row[par][c][:, :, D], top[:, :, c], gate_rcp[:], ALU.mult)
                        last = dve.tensor_copy(y_row[par][c][:, :, D + 1].bitcast(I32), token[:])
                    step(last)
                if k == 4:
                    own(n, 9)
                    step(dve.tensor_scalar(token[:], token[:], float(4 * P), None, ALU.add))
                    wait(dve, rank_ready, n + 1)
                    wait(dve, filled, n)
                    step(dve.tensor_tensor(slot_all[:], rank[:, 0:4, :], fill[:].unsqueeze(1).to_broadcast([P, 4, E]), ALU.add))
                if k == 5:
                    own(n, 11)
                    dve.tensor_tensor(fill[:], rank[:, 4, :], fill[:], ALU.add).then_inc(filled, 1)
                    for c in range(TOP_K):
                        last = dve.tensor_tensor(slot_sel[c][:], slot_all[:], chosen[c][:], ALU.mult)
                    step(last)
                if k == 6:
                    own(n, 12)
                    for c in range(TOP_K):
                        last = dve.tensor_reduce(slot_f[:, c, :], slot_sel[c][:], AX.X, ALU.add)
                    step(last)
                if k == 7:
                    own(n, 13)
                    if not (t.fixed and n < 2):
                        for c in range(TOP_K):
                            dve.wait_ge(scattered[par][c], 64 * same_parity(t, -9))
                    dve.tensor_copy(slot_idx[par][:], slot_f[:]).then_inc(slots_known, 1)

            def body(t):
                ln1 = None if t.odd else t.pair(4)
                ln2 = t.pair(-5) if t.odd else None
                zn = t.pair(3) if t.odd else None
                yn = None if t.odd else t.pair(-6)
                prep_q = t.pair(3) if t.odd else None
                prep_k = None if t.odd else t.pair(2)
                prep_v = None if t.odd else t.pair(0)
                chn = None if t.odd else t.pair(-8)
                pln = t.pair(-9) if t.odd else None
                for k in range(8):
                    if k == 6 and ln1:
                        wait(dve, bn_ready, 4 * ln1[0] + 4)
                    if k == 6 and ln2:
                        wait(dve, bn2_ready, 4 * ln2[0] + 4)
                    if k == 4 and chn:
                        own(chn[0], 2)
                    if k == 5 and chn:
                        own(chn[0], 3)
                    reduce_unit(t, k)
                    if k == 1 and zn:
                        n, par = zn
                        wait(dve, rstd_ready, n + 1)
                        wait(dve, zT_ready, n)
                        for c in range(4):
                            last = dve.tensor_scalar(z[:, c, :], tile_of(n, c), mv[:, c, 0:1], rstd[:, c:c + 1],
                                                     ALU.subtract, ALU.mult)
                        last.then_inc(z_ready, 1)
                    if k == 4 and prep_k:
                        n, par = prep_k
                        split(n, par, k_proj, k_hi, k_lo, k_lo_ready, k_hi_ready, bk_c)
                    if k == 4 and t.batch(3):
                        b, bi, slot = t.batch(3)
                        par = slot % 2
                        wait(dve, av_done, 2 * b + 2)
                        wait(dve, x1_ready, b - 1)
                        dve.transpose(att[par][:].rearrange("p g m d -> p (g m) d"),
                                      ps_av[:].rearrange("p g (u m) -> p g m u", m=8)).then_inc(att_ready, 1)
                    if k == 5 and t.batch(3):
                        wait(dve, att_ready, b + 1)
                        dve.reciprocal(rden[slot % 2][:], att[slot % 2][:, :, :, DK]).then_inc(rden_ready, 1)
                    if k == 5 and ln1:
                        n, par = ln1
                        dve.wait_ge(x_loaded[par], 16 * (same_parity(t, 4) + 1))
                        for c in range(4):
                            dve.bn_stats(bn[:, c, :], tile_of(n, c)).then_inc(bn_ready, 1)
                    if k == 6 and ln1:
                        n, par = ln1
                        for c in range(4):
                            last = dve.bn_aggr(mv[:, c, :], bn[:, c, :])
                        last.then_inc(mv_ready, 1)
                        wait(dve, mv_ready, n + 1)
                        dve.tensor_scalar(var_e[:], mv[:, :, 1], 1.0 + EPS, EPS * EPS, ALU.mult, ALU.add).then_inc(var_ready, 1)
                    if k == 5 and ln2:
                        n = ln2[0]
                        wait(dve, x1_ready, 2 * n + 2)
                        for c in range(4):
                            dve.bn_stats(bn2[:, c, :], tile_of(n, c)).then_inc(bn2_ready, 1)
                    if k == 6 and ln2:
                        n = ln2[0]
                        for c in range(4):
                            last = dve.bn_aggr(mv2[:, c, :], bn2[:, c, :])
                        last.then_inc(mv2_ready, 1)
                        wait(dve, mv2_ready, n + 1)
                        dve.tensor_scalar(var2[:], mv2[:, :, 1], EPS, None, ALU.add).then_inc(var2_ready, 1)
                    if k == 7 and prep_q:
                        n, par = prep_q
                        split(n, par, q_proj, q_hi, q_lo, q_lo_ready, q_hi_ready, bq_c)
                    if k == 7 and prep_v:
                        n, par = prep_v
                        wait(dve, v_proj, n + 1)
                        wait(dve, av_done, 4 * n - 4)
                        dve.tensor_tensor(v_aug[par][:, :, :, 0:DK],
                                          ps_mv[:].rearrange("p (c h d) -> p c h d", c=4, h=H),
                                          bv_s[:].rearrange("p (o h d) -> p o h d", o=1, h=H).to_broadcast([P, 4, H, DK]),
                                          ALU.add).then_inc(v_ready, 1)
                    if chn:
                        choose(k, *chn)
                    if pln:
                        place(k, *pln, t)
                    if k == 6 and yn:
                        n, par = yn
                        wait(dve, rstd2_ready, n + 1)
                        if not (t.fixed and n < 2):
                            dve.wait_ge(scattered[par][0], 64 * same_parity(t, -6))
                        for c in range(4):
                            last = dve.tensor_scalar(y_row[par][0][:, c, 0:D], tile_of(n, c), mv2[:, c, 0:1],
                                                     rstd2[:, c:c + 1], ALU.subtract, ALU.mult)
                        last.then_inc(y_ready, 1)

            periods(dve, body)
            made = [0]

            def make(ins):
                made[0] += 1
                ins.then_inc(tabling, 1)
                dve.wait_ge(tabling, made[0])

            def over_tiles(a):
                return a[:].unsqueeze(1).to_broadcast([P, FFN_TILES, E])

            dve.wait_ge(filled, B // 2)
            make(dve.tensor_tensor(total[:], fill[:], region[:], ALU.subtract))
            make(dve.tensor_scalar(tiles_i[:, 0, :], total[:], float(SLOTS - 1), None, ALU.add))
            make(dve.tensor_scalar(tiles_i[:, 1, :], tiles_i[:, 0, :], SLOTS.bit_length() - 1, None, ALU.arith_shift_right))
            make(dve.tensor_copy(tiles_f[:], tiles_i[:, 1, :]))
            make(dve.tensor_tensor_scan(tiles_end[:], ones_e[:], tiles_f[:], 0.0, ALU.mult, ALU.add))
            make(dve.tensor_tensor(passed[:], over_tiles(tiles_end),
                                   tile_n[:].unsqueeze(2).to_broadcast([P, FFN_TILES, E]), ALU.is_le))
            make(dve.tensor_reduce(tile_e[:], passed[:], AX.X, ALU.add))
            make(dve.tensor_tensor(passed_end[:], passed[:], over_tiles(tiles_end), ALU.mult))
            make(dve.tensor_reduce(tile_start[:], passed_end[:], AX.X, ALU.max))
            make(dve.tensor_tensor(tile_k[:], tile_n[:], tile_start[:], ALU.subtract))
            make(dve.tensor_scalar(tile_start[:], tile_e[:], float(REGION), None, ALU.mult))
            make(dve.scalar_tensor_tensor(out=tile_row[:], in0=tile_k[:], scalar=float(SLOTS), in1=tile_start[:],
                                          op0=ALU.mult, op1=ALU.add))
            make(dve.tensor_scalar(table[:, :, 0], tile_row[:], float(E * REGION), None, ALU.min))
            make(dve.tensor_scalar(table[:, :, 1], tile_e[:], float(E - 1), None, ALU.min))
            dve.tensor_copy(pad_start[:], fill[:]).then_inc(table_ready, 1)
            dve.wait_ge(table_ready, 1)

            def lo_part(lo, x, hi, s):
                dve.tensor_tensor(lo, x, hi.bitcast(F32), ALU.subtract).then_inc(s, 1)

            def hi_part(hi, x, loaded, value, s):
                dve.wait_ge(loaded, value)
                dve.tensor_copy(hi, x).then_inc(s, 1)

            def hidden_lo(t, f):
                if t.tile(0):
                    n, i, r = t.tile(0)
                    dve.wait_ge(h_hi_ready, 4 * n + f + 1)
                    lo_part(h_lo[r % 2][f], h_f32[f % 2], h_hi[r % 2][f], h_lo_ready)

            def body_b(t):
                if t.tile(-2):
                    n, i, r = t.tile(-2)
                    dve.wait_ge(o_psum, n + 1)
                    if since(n, 2):
                        dve.wait_ge(o_tok_psum, n - 1)
                    dve.tensor_scalar(oT[r % 2], ps_o[r % 2], b_cur[r][:, FC:FC + 1], None, ALU.add).then_inc(oT_ready, 1)
                if t.tile(1):
                    n, i, r = t.tile(1)
                    hi_part(w1_hi[r % 2], w1_raw[r % 2], w1_loaded[r % 2], loads(i, r, 2), w1_hi_ready)
                hidden_lo(t, 0)
                if t.tile(1):
                    n, i, r = t.tile(1)
                    dve.wait_ge(y_hi_ready, n + 1)
                    lo_part(y_lo[r % 2], ps_y, y_hi[r % 2], y_lo_ready)
                if t.tile(0):
                    n, i, r = t.tile(0)
                    hi_part(w2_hi[r % 2], w2_raw[r % 2], w2_loaded[r % 2], loads(i, r, 2), w2_hi_ready)
                hidden_lo(t, 1)
                if t.tile(1):
                    n, i, r = t.tile(1)
                    dve.wait_ge(w1_hi_ready, n + 1)
                    lo_part(w1_lo[r % 2], w1_raw[r % 2], w1_hi[r % 2], w1_lo_ready)
                if t.tile(-2):
                    n, i, r = t.tile(-2)
                    dve.wait_ge(o_tok_psum, n + 1)
                    if since(n, 2):
                        dve.wait_ge(added[r % 2], 64 * (i * 2 + r // 2))
                    dve.tensor_tensor(res[r % 2].rearrange("p (c d) -> p c d", d=D),
                                      ps_t.rearrange("p (c d) -> p c d", d=D),
                                      gate_row[r][:, :, 0:1].to_broadcast([P, SLOTS // P, D]),
                                      ALU.mult).then_inc(res_ready, 1)
                hidden_lo(t, 2)
                if t.tile(-1):
                    n, i, r = t.tile(-1)
                    if since(n, 4):
                        dve.wait_ge(added[r % 2], 64 * (i * 2 + r // 2 - 1))
                    dve.wait_ge(y_loaded[r], loads(i, r, 4))
                    dve.tensor_copy(gate_row[r][:, :, 0], y_tile[r][:, :, D])
                    dve.tensor_copy(gate_row[r][:, :, 1].bitcast(I32), y_tile[r][:, :, D + 1].bitcast(I32)).then_inc(gate_row_ready, 1)
                hidden_lo(t, 3)

            steps(dve, body_b)


_INS = ['L0_attn_x', 'L0_attn_Wq', 'L0_attn_bq', 'L0_attn_Wk', 'L0_attn_bk', 'L0_attn_Wv', 'L0_attn_bv', 'L0_attn_gamma', 'L0_attn_beta',
        'L0_ffn_centroids', 'L0_ffn_W1', 'L0_ffn_b1', 'L0_ffn_W2', 'L0_ffn_b2']


def kernel(**inputs):
    import numpy as _np
    import concourse.bacc as _bacc
    from concourse import mybir as _mybir
    from concourse.bass_utils import run_bass_kernel_spmd as _run

    nc = _bacc.Bacc("TRN2", target_bir_lowering=False, num_devices=1)
    arrays, args = {}, []
    for name in _INS:
        a = _np.ascontiguousarray(inputs[name])
        arrays[f"in_{name}_dram"] = a
        args.append(nc.dram_tensor(f"in_{name}_dram", a.shape, _mybir.dt.from_np(a.dtype), kind="ExternalInput").ap())
    args.append(nc.dram_tensor("out_0_dram", (B, S, D), F32, kind="ExternalOutput").ap())
    build(nc, *args)
    r = _run(nc, [arrays], core_ids=[0])
    return r.results[0]["out_0_dram"]
```

```python
from contextlib import ExitStack

import concourse.bass as bass
from concourse import mybir

ALU = mybir.AluOpType
ACT = mybir.ActivationFunctionType
AX = mybir.AxisListType
F32 = mybir.dt.float32
F32R = mybir.dt.float32r
BF16 = mybir.dt.bfloat16
I32 = mybir.dt.int32
U32 = mybir.dt.uint32

P = 128
B, S, D = 32, 256, 128
H = 8
DK = D // H
EPS = 1e-5
TILES = B * S // P
RING = 4
M_ROW = 96

E = 8
DFF = 4 * D
FC = DFF // P
TOP_K = 2
SLOTS = 512
ROWS = B * S
REGION = ROWS + SLOTS
FFN_TILES = (ROWS * TOP_K + E * (SLOTS - 1)) // SLOTS
WIDTH = D + 2




def build(nc, x_in, Wq, bq, Wk, bk, Wv, bv, gamma, beta, cent, W1, b1, W2, b2, out):
    with ExitStack() as ctx:
        def sb(name, shape, dt=F32):
            return ctx.enter_context(nc.sbuf_tensor(name, shape, dt))

        def sem(name):
            return ctx.enter_context(nc.semaphore(name))

        X1 = sb("X1", [P, TILES, D])
        q_stack = [sb(f"q_stack{n}", [P, H, S], F32R) for n in range(RING)]
        k_stack = [sb(f"k_stack{n}", [P, H, S], F32R) for n in range(RING)]
        probs = [sb(f"probs{n}", [P, H, 2, S]) for n in range(2)]
        v_aug = [sb(f"v_aug{n}", [P, 4, H, 32]) for n in range(2)]
        q_hi = [sb(f"q_hi{n}", [P, 512], F32R) for n in range(2)]
        q_lo = [sb(f"q_lo{n}", [P, 512], F32R) for n in range(2)]
        k_hi = [sb(f"k_hi{n}", [P, 512], F32R) for n in range(2)]
        k_lo = [sb(f"k_lo{n}", [P, 512], F32R) for n in range(2)]
        q_f32 = sb("q_f32", [P, 512])
        k_f32 = sb("k_f32", [P, 512])
        xnT = [sb(f"xnT{n}", [P, 512]) for n in range(2)]
        z = sb("z", [P, 4, D])
        row_max = [sb(f"row_max{n}", [P, 2, H]) for n in range(2)]
        neg_maxT = [sb(f"neg_maxT{n}", [H, S], F32R) for n in range(2)]
        att = [sb(f"att{n}", [P, 2, 8, 32]) for n in range(2)]
        rden = [sb(f"rden{n}", [P, 2, 8]) for n in range(2)]
        att_n = [sb(f"att_n{n}", [P, 2, 8, DK]) for n in range(2)]
        bn = sb("bn", [P, 4, 6])
        mv = sb("mv", [P, 4, 2])
        var_e = sb("var_e", [P, 4])
        neg_mean = sb("neg_mean", [P, 4])
        shift = sb("shift", [P, 4])
        rstd = sb("rstd", [P, 4])
        minus_half = sb("minus_half", [P, 4])
        gelu_first = sb("gelu_first", [P, 4])
        ident = sb("ident", [P, P])
        Wq_raw = sb("Wq_raw", [P, D])
        Wk_raw = sb("Wk_raw", [P, D])
        Wq_p = sb("Wq_p", [P, D])
        Wk_p = sb("Wk_p", [P, D])
        Wv_raw = sb("Wv_raw", [P, D * H])
        Wv_s = sb("Wv_s", [P, D])
        bv_raw = sb("bv_raw", [P, D * H])
        bv_s = sb("bv_s", [P, D])
        bq_c = sb("bq_c", [P, 1])
        bk_c = sb("bk_c", [P, 1])
        gamma_c = sb("gamma_c", [P, 1])
        beta_c = sb("beta_c", [P, 1])

        bn2 = sb("bn2", [P, 4, 6])
        mv2 = sb("mv2", [P, 4, 2])
        var2 = sb("var2", [P, 4])
        neg_mean2 = sb("neg_mean2", [P, 4])
        shift2 = sb("shift2", [P, 4])
        rstd2 = sb("rstd2", [P, 4])
        y_row = [[sb(f"y_row{n}_{k}", [P, 4, WIDTH]) for k in range(TOP_K)] for n in range(2)]
        yT = sb("yT", [P, 512])
        cent_raw = sb("cent_raw", [E, D])
        centT = sb("centT", [P, E])
        expn = sb("expn", [P, 4, E])
        den = sb("den", [P, 4, E])
        sig = sb("sig", [P, 4, E])
        top = sb("top", [P, 4, 8])
        top_e = sb("top_e", [P, 4, 8], U32)
        top_f = sb("top_f", [P, 4, TOP_K])
        chosen = [sb(f"chosen{k}", [P, 4, E]) for k in range(TOP_K)]
        gate_sum = sb("gate_sum", [P, 4])
        gate_rcp = sb("gate_rcp", [P, 4])
        picked = sb("picked", [P, 5, E], BF16)
        before = sb("before", [P, P], BF16)
        ones_bf = sb("ones_bf", [P, P], BF16)
        fill = sb("fill", [P, E])
        slot_all = sb("slot_all", [P, 4, E])
        slot_sel = [sb(f"slot_sel{k}", [P, 4, E]) for k in range(TOP_K)]
        slot_f = sb("slot_f", [P, TOP_K, 4])
        slot_idx = [sb(f"slot_idx{n}", [P, TOP_K, 4], I32) for n in range(2)]
        expert_i = sb("expert_i", [P, E], I32)
        expert_n = sb("expert_n", [P, E])
        region_i = sb("region_i", [P, E], I32)
        region = sb("region", [P, E])
        token_i = sb("token_i", [P, 4], I32)
        token = sb("token", [P, 4])
        total = sb("total", [P, E])
        tiles_i = sb("tiles_i", [P, 2, E], I32)
        tiles_f = sb("tiles_f", [P, E])
        tiles_end = sb("tiles_end", [P, E])
        ones_e = sb("ones_e", [P, E])
        tile_i = sb("tile_i", [P, FFN_TILES], I32)
        tile_n = sb("tile_n", [P, FFN_TILES])
        passed = sb("passed", [P, FFN_TILES, E])
        passed_end = sb("passed_end", [P, FFN_TILES, E])
        tile_e = sb("tile_e", [P, FFN_TILES])
        tile_start = sb("tile_start", [P, FFN_TILES])
        tile_k = sb("tile_k", [P, FFN_TILES])
        tile_row = sb("tile_row", [P, FFN_TILES])
        table = sb("table", [P, FFN_TILES, 2], I32)
        pad_start = sb("pad_start", [P, E], I32)
        pad_rows = sb("pad_rows", [P, SLOTS // P, WIDTH])
        slots = nc.dram_tensor("slots", (E * REGION + SLOTS, WIDTH), F32).ap()

        b_all = sb("b_all", [P, E, FC + 1])
        b_cur = [sb(f"b_cur{n}", [P, FC + 1]) for n in range(4)]
        tick = [sb(f"tick{n}", [P, 1]) for n in range(2)]
        gate_row = [sb(f"gate_row{n}", [P, SLOTS // P, 2]) for n in range(4)]

        ps_max = [ctx.enter_context(nc.psum_tensor(f"ps_max{n}", [P, 2, S], F32)) for n in range(2)]
        ps_st = [ctx.enter_context(nc.psum_tensor(f"ps_st{n}", [P, 2, S], F32)) for n in range(2)]
        ps_av = ctx.enter_context(nc.psum_tensor("ps_av", [P, 2, S], F32))
        ps_proj = ctx.enter_context(nc.psum_tensor("ps_proj", [P, 512], F32))
        ps_mv = ctx.enter_context(nc.psum_tensor("ps_mv", [P, 512], F32))
        ps_route = ctx.enter_context(nc.psum_tensor("ps_route", [P, 512], F32))

        norm_loaded, qk_loaded, v_loaded = sem("norm_loaded"), sem("qk_loaded"), sem("v_loaded")
        qk_ready, wv_ready = sem("qk_ready"), sem("wv_ready")
        const_ready = sem("const_ready")
        q_rest_ready, k_rest_ready = sem("q_rest_ready"), sem("k_rest_ready")
        v_rest_ready = sem("v_rest_ready")
        x_loaded = [sem(f"x_loaded{n}") for n in range(2)]
        bn_ready = sem("bn_ready")
        mv_ready = sem("mv_ready")
        var_ready = sem("var_ready")
        rstd_ready = sem("rstd_ready")
        shift_ready, shift2_ready = sem("shift_ready"), sem("shift2_ready")
        z_ready = sem("z_ready")
        zT_ready = sem("zT_ready")
        xnT_ready = sem("xnT_ready")
        q_proj, k_proj, v_proj = sem("q_proj"), sem("k_proj"), sem("v_proj")
        q_hi_ready, q_lo_ready = sem("q_hi_ready"), sem("q_lo_ready")
        k_hi_ready, k_lo_ready = sem("k_hi_ready"), sem("k_lo_ready")
        v_ready = sem("v_ready")
        stack_placed = [sem(f"stack_placed{n}") for n in range(RING)]
        m_placed = [sem(f"m_placed{n}") for n in range(RING)]
        smax_ready = sem("smax_ready")
        smax_reduced = sem("smax_reduced")
        maxT_ready = sem("maxT_ready")
        neg_maxT_ready = sem("neg_maxT_ready")
        st_ready = sem("st_ready")
        exp_done = sem("exp_done")
        av_done = sem("av_done")
        att_ready = sem("att_ready")
        rden_ready = sem("rden_ready")
        att_n_ready = sem("att_n_ready")
        x1_ready = sem("x1_ready")

        x1_stored = sem("x1_stored")
        b_loaded = sem("b_loaded")
        tabling, table_ready = sem("tabling"), sem("table_ready")
        padded = sem("padded")
        y_loaded = [sem(f"y_loaded{n}") for n in range(4)]
        w1_loaded = [sem(f"w1_loaded{n}") for n in range(2)]
        w2_loaded = [sem(f"w2_loaded{n}") for n in range(2)]
        w1_hi_ready, w1_lo_ready = sem("w1_hi_ready"), sem("w1_lo_ready")
        w2_hi_ready, w2_lo_ready = sem("w2_hi_ready"), sem("w2_lo_ready")
        b_ready = sem("b_ready")
        yT2_psum, y_hi_ready, y_lo_ready = sem("yT2_psum"), sem("y_hi_ready"), sem("y_lo_ready")
        h_psum, h_f32_ready, h_hi_ready, h_lo_ready = sem("h_psum"), sem("h_f32_ready"), sem("h_hi_ready"), sem("h_lo_ready")
        o_psum, oT_ready, o_tok_psum, res_ready = sem("o_psum"), sem("oT_ready"), sem("o_tok_psum"), sem("res_ready")
        added = [sem(f"added{n}") for n in range(2)]
        ticked = sem("ticked")
        gate_row_ready = sem("gate_row_ready")
        cent_loaded = sem("cent_loaded")
        centT_psum, centT_ready = sem("centT_psum"), sem("centT_ready")
        iota_ready = sem("iota_ready")
        floats_ready = sem("floats_ready")
        route_const = sem("route_const")
        bn2_ready, mv2_ready = sem("bn2_ready"), sem("mv2_ready")
        var2_ready, rstd2_ready = sem("var2_ready"), sem("rstd2_ready")
        y_ready, y_copied = sem("y_ready"), sem("y_copied")
        yT_psum, yT_ready = sem("yT_psum"), sem("yT_ready")
        logits_ready, expn_ready = sem("logits_ready"), sem("expn_ready")
        gating = sem("gating")
        picked_ready = sem("picked_ready")
        rank_ready = sem("rank_ready")
        filled, slots_known = sem("filled"), sem("slots_known")
        scattered = [[sem(f"scattered{n}_{k}") for k in range(TOP_K)] for n in range(2)]

        GATING = 13

        def wait(eng, s, value):
            if not isinstance(value, int) or value > 0:
                eng.wait_ge(s, value)

        class Period:

            def __init__(self, i, r):
                self.i, self.r, self.fixed = i, r, isinstance(i, int)
                self.odd = r % 2 == 1

            def batch(self, lag):
                o = self.r - lag
                b = self.i * 4 + o
                if self.fixed and not 0 <= b < B:
                    return None
                return b, self.i + o // 4, o % 4

            def pair(self, lead):
                o = self.r + lead
                assert o % 2 == 0
                n = self.i * 2 + o // 2
                if self.fixed and not 0 <= n < B // 2:
                    return None
                return n, (o // 2) % 2

        def same_parity(t, lead):
            return t.i + (t.r + lead) // 4

        def periods(eng, body):
            for j in range(-4, 12):
                body(Period(j // 4, j % 4))
            with eng.Fori(3, 7) as i:
                for r in range(4):
                    body(Period(i, r))
            for j in range(28, 40):
                body(Period(j // 4, j % 4))

        def cols(t, first, count):
            pattern = "p h t s -> p (h t s)" if len(t.shape) == 4 else "p h s -> p (h s)"
            return t[:].rearrange(pattern)[:, first * 512:(first + count) * 512]

        w1_raw = [cols(probs[0], n, 1) for n in range(2)]
        w2_raw = [cols(probs[0], 2 + n, 1) for n in range(2)]
        h_f32 = [cols(probs[1], n, 1) for n in range(2)]
        oT = [cols(probs[1], 2 + n, 1) for n in range(2)]
        res = [cols(probs[1], 4 + n, 1) for n in range(2)]
        rows = SLOTS // P * WIDTH
        y_tile = [probs[b][:].rearrange("p h t s -> p (h t s)")[:, c:c + rows].rearrange("p (c w) -> p c w", w=WIDTH)
                  for b, c in ((0, 4 * 512), (0, 4 * 512 + rows), (0, 4 * 512 + 2 * rows), (1, 6 * 512))]
        w1_hi = [cols(q_stack[0], n, 1) for n in range(2)]
        w2_hi = [cols(q_stack[0], 2 + n, 1) for n in range(2)]
        w1_lo = [cols(q_stack[1], n, 1) for n in range(2)]
        w2_lo = [cols(q_stack[1], 2 + n, 1) for n in range(2)]
        y_hi = [cols(q_stack[2], n, 1) for n in range(2)]
        y_lo = [cols(q_stack[2], 2 + n, 1) for n in range(2)]
        h_hi = [[cols(k_stack[n], f, 1) for f in range(FC)] for n in range(2)]
        h_lo = [[cols(k_stack[2 + n], f, 1) for f in range(FC)] for n in range(2)]
        ps_h = [ps_st[n][:].rearrange("p a s -> p (a s)") for n in range(2)] + [ps_proj[:], ps_mv[:]]
        ps_o = [ps_max[n][:].rearrange("p a s -> p (a s)") for n in range(2)]
        ps_y = ps_av[:].rearrange("p a s -> p (a s)")
        ps_t = ps_route[:]

        class Step:

            def __init__(self, i, r):
                self.i, self.r, self.fixed = i, r, isinstance(i, int)

            def tile(self, lead):
                o = self.r + lead
                n = self.i * 4 + o
                if self.fixed and not 0 <= n < FFN_TILES:
                    return None
                return n, self.i + o // 4, o % 4

        def steps(eng, body):
            last = (FFN_TILES - 3) // 4
            for t in range(-2, 4):
                body(Step(t // 4, t % 4))
            with eng.Fori(1, last) as i:
                for r in range(4):
                    body(Step(i, r))
            for t in range(4 * last, FFN_TILES + 2):
                body(Step(t // 4, t % 4))

        def since(n, back):
            return not isinstance(n, int) or n >= back

        def loads(i, r, ring):
            return 16 * (i + 1) if ring == 4 else 16 * (i * 2 + r // 2 + 1)

        def tile_of(n, c):
            return X1[:, bass.ds(n * 4 + c, 1), :].rearrange("p o d -> p (o d)")

        def pad(eng, experts):
            for e in experts:
                start = eng.value_load(pad_start[0:1, e:e + 1], min_val=e * REGION, max_val=e * REGION + ROWS)
                eng.dma_start(slots[bass.ds(start, SLOTS), :].rearrange("(c p) w -> p c w", p=P),
                              pad_rows[:]).then_inc(padded, 16)

        block = ctx.enter_context(nc.Block())

        @block.sync
        def _(sp):
            xt = x_in.rearrange("b (c p) d -> p (b c) d", p=P)
            out_t = out.rearrange("b (c p) d -> p (b c) d", p=P)

            def load_x(n, par):
                sp.dma_start(X1[:, bass.ds(n * 4, 4), :], xt[:, bass.ds(n * 4, 4), :]).then_inc(x_loaded[par], 16)

            load_x(0, 0)
            sp.dma_start(cent_raw[:], cent).then_inc(cent_loaded, 16)
            sp.dma_start(gamma_c[:], gamma.rearrange("(p o) -> p o", o=1)).then_inc(norm_loaded, 16)
            sp.dma_start(beta_c[:], beta.rearrange("(p o) -> p o", o=1)).then_inc(norm_loaded, 16)
            sp.dma_start(Wq_raw[:], Wq).then_inc(qk_loaded, 16)
            sp.dma_start(bq_c[:], bq.rearrange("(h d o) -> d h o", h=H, o=1), allow_slow_non_contiguous=True).then_inc(qk_loaded, 16)
            sp.dma_start(Wk_raw[:], Wk).then_inc(qk_loaded, 16)
            sp.dma_start(bk_c[:], bk.rearrange("(h d o) -> d h o", h=H, o=1), allow_slow_non_contiguous=True).then_inc(qk_loaded, 16)
            load_x(1, 1)
            sp.dma_start(Wv_raw[:], Wv).then_inc(v_loaded, 16)
            sp.dma_start(bv_raw[:], bv.rearrange("(o n) -> o n", o=1).broadcast_to([P, D * H])).then_inc(v_loaded, 16)

            def body(t):
                if not t.odd:
                    p = t.pair(4)
                    if p and not (t.fixed and p[0] < 2):
                        wait(sp, bn_ready, 4 * (p[0] - 1))
                        load_x(*p)
                nb = t.batch(-1)
                if nb:
                    b, bi, slot = nb
                    n = bi * 2 + slot // 2
                    par = (slot // 2) % 2
                    wait(sp, q_lo_ready, n + 1)
                    wait(sp, k_lo_ready, n + 1)
                    if t.fixed and b < RING:
                        sp.wait_ge(q_rest_ready, b + 1)
                        sp.wait_ge(k_rest_ready, b + 1)
                    wait(sp, st_ready, 8 * b - 24)
                    half = slice((slot % 2) * S, (slot % 2) * S + S)
                    for part, (qs, ks) in enumerate(((q_hi, k_hi), (q_lo, k_hi), (q_hi, k_lo))):
                        for stack, src in ((q_stack, qs), (k_stack, ks)):
                            sp.dma_start(
                                stack[slot][part * DK:(part + 1) * DK, :, :].rearrange("p h s -> p (h s)").bitcast(F32),
                                src[par][:, half].bitcast(F32)).then_inc(stack_placed[slot], 16)
                nb = t.batch(4)
                if nb:
                    b = nb[0]
                    wait(sp, x1_ready, b + 1)
                    sp.dma_start(out_t[:, bass.ds(b * 2, 2), :], X1[:, bass.ds(b * 2, 2), :]).then_inc(x1_stored, 16)

            for f in range(FC):
                sp.dma_start(b_all[:, :, f:f + 1], b1.rearrange("e (f p o) -> f p e o", p=P, o=1)[f],
                             allow_slow_non_contiguous=True).then_inc(b_loaded, 16)
            sp.dma_start(b_all[:, :, FC:FC + 1], b2.rearrange("e (p o) -> p e o", o=1),
                         allow_slow_non_contiguous=True).then_inc(b_loaded, 16)
            periods(sp, body)
            sp.wait_ge(table_ready, 1)

            def load_w(n, r, w, dst, loaded, free):
                e = sp.value_load(table[0:1, bass.ds(n, 1), 1:2].rearrange("p a b -> p (a b)"), min_val=0, max_val=E - 1)
                if since(n, 2):
                    sp.wait_ge(free, n - 1)
                sp.dma_start(dst, w(e)).then_inc(loaded[r % 2], 16)

            def load_w1(n, i, r):
                load_w(n, r, lambda e: W1[bass.ds(e, 1)].rearrange("e d f -> d (e f)"), w1_raw[r % 2], w1_loaded, w1_lo_ready)

            def load_w2(n, i, r):
                load_w(n, r, lambda e: W2[bass.ds(e, 1)].rearrange("e (f p) d -> p (e f) d", p=P),
                       w2_raw[r % 2].rearrange("p (f d) -> p f d", f=FC), w2_loaded, w2_lo_ready)

            load_w1(0, 0, 0)
            pad(sp, range(E // 2, E))
            load_w2(0, 0, 0)
            load_w1(1, 0, 1)
            sp.dma_start(slots.rearrange("(c p) w -> p c w", p=P)[:, E * REGION // P:, :], pad_rows[:]).then_inc(padded, 16)

            def load(t):
                if t.tile(2):
                    n, i, r = t.tile(2)
                    row = sp.value_load(table[0:1, bass.ds(n, 1), 0:1].rearrange("p a b -> p (a b)"), min_val=0, max_val=E * REGION)
                    if not since(n, 1):
                        sp.wait_ge(padded, 16 * (E + 1))
                        for m in range(2):
                            for k in range(TOP_K):
                                sp.wait_ge(scattered[m][k], 64 * B // 4)
                    if since(n, 4):
                        sp.wait_ge(yT2_psum, n - 3)
                        sp.wait_ge(gate_row_ready, n - 3)
                    sp.dma_start(y_tile[r], slots[bass.ds(row, SLOTS), :].rearrange("(c p) w -> p c w", p=P)).then_inc(y_loaded[r], 16)
                    if since(n, 2):
                        load_w1(n, i, r)
                if t.tile(1) and since(t.tile(1)[0], 1):
                    load_w2(*t.tile(1))

            steps(sp, load)

        @block.gpsimd
        def _(pool):
            pool.memset(minus_half[:], -0.5).then_inc(const_ready, 1)
            pool.memset(ident[:], 0.0).then_inc(const_ready, 1)
            pool.wait_ge(const_ready, 2)
            pool.affine_select(out=ident[:], in_=ident[:], compare_op=ALU.not_equal, fill=1.0, base=0,
                               pattern=[[-1, P]], channel_multiplier=1).then_inc(const_ready, 1)

            def set_stack(n):
                pool.memset(k_stack[n][:].bitcast(F32), 1.0).then_inc(k_rest_ready, 1)

            def set_v_and_route():
                for n in range(2):
                    pool.memset(v_aug[n][:], 1.0).then_inc(v_rest_ready, 1)
                pool.iota(expert_i[:], pattern=[[1, E]], base=0, channel_multiplier=0).then_inc(iota_ready, 1)
                pool.iota(region_i[:], pattern=[[REGION, E]], base=0, channel_multiplier=0).then_inc(iota_ready, 1)
                pool.iota(token_i[:], pattern=[[P, 4]], base=0, channel_multiplier=1).then_inc(iota_ready, 1)
                pool.iota(tile_i[:], pattern=[[1, FFN_TILES]], base=0, channel_multiplier=0).then_inc(iota_ready, 1)
                pool.memset(ones_bf[:], 1.0).then_inc(route_const, 1)
                pool.memset(ones_e[:], 1.0).then_inc(route_const, 1)
                pool.memset(picked[:], 0.0).then_inc(route_const, 1)
                pool.memset(pad_rows[:], 0.0).then_inc(route_const, 1)
                pool.memset(tick[0][:], 0.0).then_inc(route_const, 1)
                pool.wait_ge(route_const, 5)
                pool.affine_select(out=before[:], in_=ones_bf[:], compare_op=ALU.is_gt, fill=0.0, base=0,
                                   pattern=[[1, P]], channel_multiplier=-1).then_inc(route_const, 1)
                pool.memset(pad_rows[:, :, D + 1].bitcast(I32), 2 * ROWS).then_inc(route_const, 1)

            def lo_part(n, par, x, hi, lo, hi_ready, lo_ready):
                wait(pool, hi_ready, n + 1)
                pool.tensor_tensor(lo[par][:], x[:], hi[par][:].bitcast(F32), ALU.subtract).then_inc(lo_ready, 1)

            def body(t):
                ln1 = None if t.odd else t.pair(4)
                ln2 = t.pair(-5) if t.odd else None
                if ln1:
                    wait(pool, var_ready, ln1[0] + 1)
                    wait(pool, z_ready, ln1[0])
                    pool.tensor_tensor(rstd[:], var_e[:], minus_half[:], ALU.pow).then_inc(rstd_ready, 1)
                    wait(pool, rstd_ready, ln1[0] + 1)
                    pool.tensor_tensor(shift[:], neg_mean[:], rstd[:], ALU.mult).then_inc(shift_ready, 1)
                if not t.odd and t.pair(2):
                    n, par = t.pair(2)
                    lo_part(n, par, k_f32, k_hi, k_lo, k_hi_ready, k_lo_ready)
                nb = t.batch(3)
                if nb:
                    b, bi, slot = nb
                    par = slot % 2
                    wait(pool, rden_ready, b + 1)
                    pool.tensor_tensor(att_n[par][:], att[par][:, :, :, 0:DK],
                                       rden[par][:].unsqueeze(3).to_broadcast([P, 2, 8, DK]),
                                       ALU.mult).then_inc(att_n_ready, 1)
                    wait(pool, att_n_ready, b + 1)
                    xs = X1[:, bass.ds(b * 2, 2), :]
                    pool.tensor_tensor(xs, xs, att_n[par][:].rearrange("p g m d -> p g (m d)"),
                                       ALU.add).then_inc(x1_ready, 1)
                if t.odd and t.pair(3):
                    n, par = t.pair(3)
                    lo_part(n, par, q_f32, q_hi, q_lo, q_hi_ready, q_lo_ready)
                if ln2:
                    wait(pool, var2_ready, ln2[0] + 1)
                    wait(pool, y_ready, ln2[0])
                    pool.tensor_tensor(rstd2[:], var2[:], minus_half[:], ALU.pow).then_inc(rstd2_ready, 1)
                    wait(pool, rstd2_ready, ln2[0] + 1)
                    pool.tensor_tensor(shift2[:], neg_mean2[:], rstd2[:], ALU.mult).then_inc(shift2_ready, 1)
                k, pr = (1, t.pair(-9)) if t.odd else (0, t.pair(-8))
                if pr and not t.odd:
                    wait(pool, slots_known, pr[0] + 1)
                    wait(pool, ticked, pr[0])
                    pool.tensor_tensor(tick[1][:], tick[0][:], tick[0][:], ALU.add).then_inc(ticked, 1)
                if pr:
                    n, par_s = pr
                    for c in range(4):
                        pool.indirect_dma_start(slots, bass.IndirectOffsetOnAxis(slot_idx[par_s][:, k, c:c + 1], 0),
                                                y_row[par_s][k][:, c, :], None).then_inc(scattered[par_s][k], 16)
                if t.fixed and t.i == -1:
                    set_stack(t.r)
                    if t.r == RING - 1:
                        set_v_and_route()

            periods(pool, body)
            out_rows = out.rearrange("b s d -> (b s) d")
            pool.wait_ge(table_ready, 1)

            pool.wait_ge(x1_stored, 16 * B)
            last_row = pool.to_reg(ROWS - 1)

            def expert(t):
                if t.tile(1):
                    n, i, r = t.tile(1)
                    e = pool.value_load(table[0:1, bass.ds(n, 1), 1:2].rearrange("p a b -> p (a b)"), min_val=0, max_val=E - 1)
                    if since(n, 4):
                        pool.wait_ge(oT_ready, n - 3)
                    pool.wait_ge(b_loaded, 16 * (FC + 1))
                    pool.tensor_copy(b_cur[r][:], b_all[:, bass.ds(e, 1), :].rearrange("p a b -> p (a b)")).then_inc(b_ready, 1)
                if t.tile(0):
                    n, i, r = t.tile(0)
                    pool.wait_ge(w2_hi_ready, n + 1)
                    if since(n, 2):
                        pool.wait_ge(o_psum, n - 1)
                    pool.tensor_tensor(w2_lo[r % 2], w2_raw[r % 2], w2_hi[r % 2].bitcast(F32), ALU.subtract).then_inc(w2_lo_ready, 1)
                if t.tile(-2):
                    n, i, r = t.tile(-2)
                    par = r % 2
                    pool.wait_ge(res_ready, n + 1)
                    if since(n, 1):
                        o = r - 1
                        pool.wait_ge(added[o % 2], 64 * ((i + o // 4) * 2 + (o % 4) // 2 + 1))
                    pool.wait_ge(gate_row_ready, n + 1)
                    pool.wait_ge(ticked, B // 2 + n)
                    pool.tensor_tensor(tick[1][:], tick[0][:], tick[0][:], ALU.add).then_inc(ticked, 1)
                    for c in range(SLOTS // P):
                        pool.indirect_dma_start(
                            out_rows, bass.IndirectOffsetOnAxis(gate_row[r][:, c, 1:2].bitcast(I32), 0),
                            res[par][:, c * P:(c + 1) * P], None, bounds_check=last_row, oob_is_err=False,
                            compute_op=ALU.add).then_inc(added[par], 16)

            steps(pool, expert)
            pool.wait_ge(added[0], 64 * ((FFN_TILES + 1) // 2))
            pool.wait_ge(added[1], 64 * (FFN_TILES // 2))

        @block.scalar
        def _(act):
            act.wait_ge(centT_psum, 1)
            act.activation(centT[:], ps_route[:, 0:E], ACT.Copy).then_inc(centT_ready, 1)
            act.wait_ge(qk_loaded, 4 * 16)
            act.activation(Wq_p[:].rearrange("p (d h) -> p d h", h=H),
                           Wq_raw[:].rearrange("p (h d) -> p d h", h=H), ACT.Copy).then_inc(qk_ready, 1)
            act.activation(Wk_p[:].rearrange("p (d h) -> p d h", h=H),
                           Wk_raw[:].rearrange("p (h d) -> p d h", h=H), ACT.Copy).then_inc(qk_ready, 1)
            act.wait_ge(norm_loaded, 2 * 16)

            def exps(t, h):
                nb = t.batch(2)
                if nb:
                    b, bi, slot = nb
                    if h == 0:
                        wait(act, av_done, 2 * b - 2)
                    wait(act, st_ready, 8 * b + h + 1)
                    act.activation(probs[slot % 2][:, h, :, :], ps_st[h % 2][:], ACT.Exp,
                                   scale=DK ** -0.5).then_inc(exp_done, 1)

            def body(t):
                prep = t.pair(3) if t.odd else None
                prep_k = None if t.odd else t.pair(2)
                ry = None if t.odd else t.pair(-6)
                rl = t.pair(-7) if t.odd else None
                for h in range(H):
                    exps(t, h)
                    if h in (0, 1) and prep:
                        n = prep[0]
                        if h == 0:
                            wait(act, shift_ready, n + 1)
                            wait(act, zT_ready, n)
                        for c in range(2 * h, 2 * h + 2):
                            last = act.activation(z[:, c, :], tile_of(n, c), ACT.Identity, bias=shift[:, c:c + 1],
                                                  scale=rstd[:, c:c + 1])
                        if h == 1:
                            last.then_inc(z_ready, 1)
                    if h in (1, 2) and ry:
                        ny, py = ry
                        if h == 1:
                            wait(act, shift2_ready, ny + 1)
                            if not (t.fixed and ny < 2):
                                act.wait_ge(scattered[py][0], 64 * same_parity(t, -6))
                        for c in range(2 * h - 2, 2 * h):
                            last = act.activation(y_row[py][0][:, c, 0:D], tile_of(ny, c), ACT.Identity,
                                                  bias=shift2[:, c:c + 1], scale=rstd2[:, c:c + 1])
                        if h == 2:
                            last.then_inc(y_ready, 1)
                    if h == 1 and rl:
                        wait(act, logits_ready, rl[0] + 1)
                        wait(act, gating, GATING * rl[0])
                        act.activation(expn[:], ps_route[:, 0:4 * E].rearrange("p (c e) -> p c e", e=E), ACT.Exp,
                                       scale=-1.0).then_inc(expn_ready, 1)
                    if h == 1 and t.batch(1):
                        b, bi, slot = t.batch(1)
                        wait(act, maxT_ready, b + 1)
                        if not (t.fixed and b < 2):
                            o = slot - 2
                            act.wait_ge(m_placed[o % 4], 16 * (bi + o // 4 + 1))
                        act.activation(neg_maxT[slot % 2][:], ps_mv[0:H, 0:S], ACT.Copy, scale=-1.0).then_inc(neg_maxT_ready, 1)
                    if h == 2 and t.batch(1):
                        b, bi, slot = t.batch(1)
                        wait(act, neg_maxT_ready, b + 1)
                        act.wait_ge(stack_placed[slot], 96 * (bi + 1))
                        act.dma_start(q_stack[slot][M_ROW:M_ROW + 1, :, :].rearrange("p h s -> p (h s)").bitcast(F32),
                                      neg_maxT[slot % 2][:].bitcast(F32)).then_inc(m_placed[slot], 16)
                    if h == 2 and prep_k:
                        n, par = prep_k
                        wait(act, k_proj, n + 1)
                        wait(act, k_lo_ready, n)
                        act.activation(k_f32[:], ps_proj[:], ACT.Identity, bias=bk_c[:, 0:1])
                        act.activation(k_hi[par][:], ps_proj[:], ACT.Identity, bias=bk_c[:, 0:1]).then_inc(k_hi_ready, 1)
                    if h == 3 and prep:
                        n, par = prep
                        wait(act, zT_ready, n + 1)
                        wait(act, v_proj, n - 1)
                        act.activation(xnT[par][:], ps_proj[:], ACT.Identity, bias=beta_c[:, 0:1],
                                       scale=gamma_c[:, 0:1]).then_inc(xnT_ready, 1)
                    if h == 5 and prep:
                        n, par = prep
                        wait(act, q_proj, n + 1)
                        if not (t.fixed and n < 2):
                            for o in (t.r + 3 - 4, t.r + 3 - 3):
                                act.wait_ge(stack_placed[o % 4], 96 * (t.i + o // 4 + 1))
                        wait(act, q_lo_ready, n)
                        act.activation(q_f32[:], ps_proj[:], ACT.Identity, bias=bq_c[:, 0:1])
                        act.activation(q_hi[par][:], ps_proj[:], ACT.Identity, bias=bq_c[:, 0:1]).then_inc(q_hi_ready, 1)
                    if h == 5 and ry:
                        ny, py = ry
                        wait(act, yT_psum, ny + 1)
                        act.activation(yT[:], ps_route[:], ACT.Copy).then_inc(yT_ready, 1)
                    if h == 7 and ry:
                        wait(act, y_ready, ny + 1)
                        if not (t.fixed and ny < 2):
                            act.wait_ge(scattered[py][1], 64 * same_parity(t, -6))
                        act.activation(y_row[py][1][:, :, 0:D], y_row[py][0][:, :, 0:D], ACT.Copy).then_inc(y_copied, 1)

            periods(act, body)
            act.wait_ge(table_ready, 1)
            pad(act, range(E // 2))
            act.activation(gelu_first[:], minus_half[:], ACT.Gelu)

            def hidden(t, f):
                if t.tile(0):
                    n, i, r = t.tile(0)
                    par = r % 2
                    if f == 0:
                        act.wait_ge(b_ready, n + 1)
                    act.wait_ge(h_psum, 4 * n + f + 1)
                    if not (t.fixed and 4 * n + f < 2):
                        act.wait_ge(h_lo_ready, 4 * n + f - 1)
                    act.activation(h_f32[f % 2], ps_h[f], ACT.Gelu, bias=b_cur[r][:, f:f + 1]).then_inc(h_f32_ready, 1)
                    if f == 0 and since(n, 2):
                        act.wait_ge(o_psum, n - 1)
                    act.activation(h_hi[par][f], ps_h[f], ACT.Gelu, bias=b_cur[r][:, f:f + 1]).then_inc(h_hi_ready, 1)

            def body_b(t):
                hidden(t, 0)
                if t.tile(1):
                    n, i, r = t.tile(1)
                    act.wait_ge(yT2_psum, n + 1)
                    act.activation(y_hi[r % 2], ps_y, ACT.Copy).then_inc(y_hi_ready, 1)
                hidden(t, 1)
                hidden(t, 2)
                hidden(t, 3)

            steps(act, body_b)

        @block.tensor
        def _(pe):
            pe.wait_ge(const_ready, 3)
            pe.wait_ge(cent_loaded, 16)
            pe.transpose(ps_route[:, 0:E], cent_raw[:], ident[0:E, 0:E]).then_inc(centT_psum, 1)

            def max_unit(t, k):
                nb = t.batch(0)
                if nb:
                    b, bi, slot = nb
                    if k == 0:
                        pe.wait_ge(stack_placed[slot], 96 * (bi + 1))
                    sc, hp = k // 4, k % 4
                    wait(pe, smax_reduced, 8 * b + k - 1)
                    for hh in range(2):
                        h = 2 * hp + hh
                        last = pe.matmul(ps_max[k % 2][:, hh, :], q_stack[slot][0:M_ROW, h, sc * P:(sc + 1) * P],
                                         k_stack[slot][0:M_ROW, h, :], start=True, stop=True)
                    last.then_inc(smax_ready, 1)

            def st_unit(t, h):
                nb = t.batch(2)
                if nb:
                    b, bi, slot = nb
                    if h == 0:
                        pe.wait_ge(m_placed[slot], 16 * (bi + 1))
                    wait(pe, exp_done, 8 * b + h - 1)
                    for tc in range(2):
                        last = pe.matmul(ps_st[h % 2][:, tc, :], k_stack[slot][:, h, tc * P:(tc + 1) * P],
                                         q_stack[slot][:, h, :], start=True, stop=True)
                    last.then_inc(st_ready, 1)

            def av(t, lag, g):
                nb = t.batch(lag)
                if nb:
                    b, bi, slot = nb
                    n = bi * 2 + slot // 2
                    if g == 0:
                        if t.fixed and b == 0:
                            pe.wait_ge(v_rest_ready, 2)
                        wait(pe, v_ready, n + 1)
                        wait(pe, att_ready, b)
                    wait(pe, exp_done, 8 * b + 4 * g + 4)
                    for tc in range(2):
                        for j in range(4):
                            h = 4 * g + j
                            last = pe.matmul(ps_av[32 * j:32 * j + 32, g, :],
                                             v_aug[(slot // 2) % 2][:, 2 * (slot % 2) + tc, h, :],
                                             probs[slot % 2][:, h, tc, :], start=(tc == 0), stop=(tc == 1),
                                             tile_position=(0, 32 * j))
                    last.then_inc(av_done, 1)

            def body(t):
                prep = t.pair(3) if t.odd else None
                prep_k = None if t.odd else t.pair(2)
                prep_v = None if t.odd else t.pair(0)
                rank_n = None if t.odd else t.pair(-8)
                route = None if t.odd else t.pair(-6)
                logits_n = t.pair(-7) if t.odd else None
                for k in range(8):
                    max_unit(t, k)
                    st_unit(t, k)
                    if k == 1 and t.batch(1):
                        b, bi, slot = t.batch(1)
                        wait(pe, smax_reduced, 8 * b + 8)
                        wait(pe, neg_maxT_ready, b)
                        if t.odd and t.pair(-1):
                            wait(pe, v_ready, t.pair(-1)[0] + 1)
                        for sc in range(2):
                            last = pe.transpose(ps_mv[0:H, sc * P:(sc + 1) * P], row_max[slot % 2][:, sc, :], ident[:])
                        last.then_inc(maxT_ready, 1)
                    if k == 2 and prep_k:
                        n, par = prep_k
                        wait(pe, q_hi_ready, n + 1)
                        pe.matmul(ps_proj[:], Wk_p[:], xnT[par][:], start=True, stop=True).then_inc(k_proj, 1)
                    if k == 2 and rank_n:
                        if t.fixed and rank_n[0] == 0:
                            pe.wait_ge(route_const, 7)
                        wait(pe, picked_ready, rank_n[0] + 1)
                        rank = ps_route[:, 0:5 * E]
                        pe.matmul(rank, before[:], picked[:].rearrange("p c e -> p (c e)"), start=True, stop=False)
                        for c in range(4):
                            last = pe.matmul(rank[:, (c + 1) * E:5 * E], ones_bf[:],
                                             picked[:, c:c + 1, :].to_broadcast([P, 4 - c, E]),
                                             start=False, stop=(c == 3))
                        last.then_inc(rank_ready, 1)
                    if k == 3 and prep:
                        n, par = prep
                        wait(pe, z_ready, n + 1)
                        wait(pe, k_hi_ready, n)
                        for c in range(4):
                            last = pe.transpose(ps_proj[:, c * P:(c + 1) * P], z[:, c, :], ident[:])
                        last.then_inc(zT_ready, 1)
                    if k == 5 and prep:
                        n, par = prep
                        if t.fixed and n == 0:
                            pe.wait_ge(qk_ready, 2)
                        wait(pe, xnT_ready, n + 1)
                        pe.matmul(ps_proj[:], Wq_p[:], xnT[par][:], start=True, stop=True).then_inc(q_proj, 1)
                    if k == 5 and route:
                        ny, py = route
                        wait(pe, y_ready, ny + 1)
                        if rank_n:
                            wait(pe, filled, rank_n[0] + 1)
                        elif ny > 0:
                            wait(pe, expn_ready, ny)
                        for c in range(4):
                            last = pe.transpose(ps_route[:, c * P:(c + 1) * P], y_row[py][0][:, c, 0:D], ident[:])
                        last.then_inc(yT_psum, 1)
                    if k == 0 and logits_n:
                        wait(pe, yT_ready, logits_n[0] + 1)
                        for c in range(4):
                            last = pe.matmul(ps_route[:, c * E:(c + 1) * E], yT[:, c * P:(c + 1) * P], centT[:],
                                             start=True, stop=True)
                        last.then_inc(logits_ready, 1)
                    if k == 4 and prep_v:
                        n, par = prep_v
                        if t.fixed and n == 0:
                            pe.wait_ge(wv_ready, 2)
                        if t.batch(1):
                            wait(pe, neg_maxT_ready, t.batch(1)[0] + 1)
                        for c in range(4):
                            last = pe.matmul(ps_mv[:, c * P:(c + 1) * P], xnT[par][:, c * P:(c + 1) * P], Wv_s[:],
                                             start=True, stop=True)
                        last.then_inc(v_proj, 1)
                    if k == 2:
                        av(t, 3, 1)
                    if k == 7:
                        av(t, 2, 0)

            periods(pe, body)
            pe.wait_ge(table_ready, 1)

            def three(o, w_hi, w_lo, x_hi, x_lo, start, stop):
                pe.matmul(o, w_hi, x_hi, start=start, stop=False)
                pe.matmul(o, w_lo, x_hi, start=False, stop=False)
                return pe.matmul(o, w_hi, x_lo, start=False, stop=stop)

            def body_b(t):
                for f in range(FC):
                    part = slice(f * P, (f + 1) * P)
                    if t.tile(0):
                        n, i, r = t.tile(0)
                        par = r % 2
                        if f == 0:
                            pe.wait_ge(w1_hi_ready, n + 1)
                            pe.wait_ge(w1_lo_ready, n + 1)
                            pe.wait_ge(y_lo_ready, n + 1)
                        if since(n, 1):
                            pe.wait_ge(h_hi_ready, 4 * (n - 1) + f + 1)
                        three(ps_h[f], w1_hi[par][:, part], w1_lo[par][:, part], y_hi[par], y_lo[par],
                              True, True).then_inc(h_psum, 1)
                    if t.tile(-1):
                        n, i, r = t.tile(-1)
                        par = r % 2
                        if f == 0:
                            pe.wait_ge(w2_hi_ready, n + 1)
                            pe.wait_ge(w2_lo_ready, n + 1)
                            if since(n, 2):
                                pe.wait_ge(oT_ready, n - 1)
                        pe.wait_ge(h_lo_ready, 4 * n + f + 1)
                        last = three(ps_o[par], w2_hi[par][:, part], w2_lo[par][:, part], h_hi[par][f], h_lo[par][f],
                                     f == 0, f == FC - 1)
                        if f == FC - 1:
                            last.then_inc(o_psum, 1)
                    if f == 1 and t.tile(-2):
                        n, i, r = t.tile(-2)
                        pe.wait_ge(oT_ready, n + 1)
                        if since(n, 1):
                            pe.wait_ge(res_ready, n)
                        for c in range(SLOTS // P):
                            last = pe.transpose(ps_t[:, c * P:(c + 1) * P], oT[r % 2][:, c * P:(c + 1) * P], ident[:])
                        last.then_inc(o_tok_psum, 1)
                    if f == 0 and t.tile(1):
                        n, i, r = t.tile(1)
                        pe.wait_ge(y_loaded[r], loads(i, r, 4))
                        if since(n, 1):
                            pe.wait_ge(y_lo_ready, n)
                        for c in range(SLOTS // P):
                            last = pe.transpose(ps_y[:, c * P:(c + 1) * P], y_tile[r][:, c, 0:D], ident[:])
                        last.then_inc(yT2_psum, 1)

            steps(pe, body_b)

        @block.vector
        def _(dve):
            dve.memset(q_stack[0][:].bitcast(F32), 0.0).then_inc(q_rest_ready, 1)

            def set_up(r):
                for n in (1, 2) if r == 1 else (3,):
                    dve.memset(q_stack[n][:].bitcast(F32), 0.0).then_inc(q_rest_ready, 1)
                if r == 3:
                    dve.wait_ge(v_loaded, 2 * 16)
                    dve.tensor_reduce(Wv_s[:], Wv_raw[:].rearrange("p (n g) -> p n g", g=8), AX.X, ALU.add).then_inc(wv_ready, 1)
                    dve.tensor_reduce(bv_s[:], bv_raw[:].rearrange("p (n g) -> p n g", g=8), AX.X, ALU.add).then_inc(wv_ready, 1)

            def reduce_unit(t, k):
                nb = t.batch(0)
                if nb:
                    b, bi, slot = nb
                    if k == 0:
                        wait(dve, maxT_ready, b - 1)
                    sc, hp = k // 4, k % 4
                    wait(dve, smax_ready, 8 * b + k + 1)
                    dve.tensor_reduce(row_max[slot % 2][:, sc, 2 * hp:2 * hp + 2], ps_max[k % 2][:], AX.X,
                                      ALU.max).then_inc(smax_reduced, 1)

            def own(n, count):
                wait(dve, gating, GATING * n + count)

            def step(ins):
                ins.then_inc(gating, 1)

            def over_e(a):
                return a[:].unsqueeze(2).to_broadcast([P, 4, E])

            def choose(k, n, par):
                if k == 2:
                    wait(dve, expn_ready, n + 1)
                    step(dve.tensor_scalar(den[:], expn[:], 1.0, None, ALU.add))
                if k == 3:
                    own(n, 1)
                    step(dve.reciprocal(sig[:], den[:]))
                if k == 4:
                    for c in range(4):
                        last = dve.max(top[:, c, :], sig[:, c, :])
                    step(last)
                if k == 5:
                    for c in range(4):
                        last = dve.max_index(top_e[:, c, :], top[:, c, :], sig[:, c, :])
                    step(last)
                if k == 6:
                    own(n, 4)
                    step(dve.tensor_copy(top_f[:], top_e[:, :, 0:TOP_K]))
                if k == 7:
                    own(n, 5)
                    for c in range(TOP_K):
                        last = dve.tensor_tensor(chosen[c][:], expert_n[:].unsqueeze(1).to_broadcast([P, 4, E]),
                                                 top_f[:, :, c:c + 1].to_broadcast([P, 4, E]), ALU.is_equal)
                    step(last)

            def place(k, n, par, t):
                rank = ps_route[:, 0:5 * E].rearrange("p (c e) -> p c e", e=E)
                if k == 0:
                    own(n, 6)
                    wait(dve, rank_ready, n)
                    dve.tensor_tensor(picked[:, 0:4, :], chosen[0][:], chosen[1][:], ALU.add).then_inc(picked_ready, 1)
                    step(dve.tensor_tensor(gate_sum[:], top[:, :, 0], top[:, :, 1], ALU.add))
                if k == 2:
                    own(n, 7)
                    step(dve.reciprocal(gate_rcp[:], gate_sum[:]))
                if k == 3:
                    wait(dve, rank_ready, n + 1)
                    wait(dve, filled, n)
                    step(dve.tensor_tensor(slot_all[:], rank[:, 0:4, :], fill[:].unsqueeze(1).to_broadcast([P, 4, E]), ALU.add))
                    own(n, 9)
                    dve.tensor_tensor(fill[:], rank[:, 4, :], fill[:], ALU.add).then_inc(filled, 1)
                if k == 4:
                    wait(dve, y_copied, n + 1)
                    for c in range(TOP_K):
                        dve.tensor_tensor(y_row[par][c][:, :, D], top[:, :, c], gate_rcp[:], ALU.mult)
                        last = dve.tensor_copy(y_row[par][c][:, :, D + 1].bitcast(I32), token[:])
                    step(last)
                if k == 5:
                    own(n, 10)
                    step(dve.tensor_scalar(token[:], token[:], float(4 * P), None, ALU.add))
                    for c in range(TOP_K):
                        last = dve.tensor_tensor(slot_sel[c][:], slot_all[:], chosen[c][:], ALU.mult)
                    step(last)
                if k == 6:
                    own(n, 12)
                    for c in range(TOP_K):
                        last = dve.tensor_reduce(slot_f[:, c, :], slot_sel[c][:], AX.X, ALU.add)
                    step(last)
                if k == 7:
                    own(n, 13)
                    if not (t.fixed and n < 2):
                        for c in range(TOP_K):
                            dve.wait_ge(scattered[par][c], 64 * same_parity(t, -8))
                    dve.tensor_copy(slot_idx[par][:], slot_f[:]).then_inc(slots_known, 1)

            def body(t):
                ln1 = None if t.odd else t.pair(4)
                ln2 = t.pair(-5) if t.odd else None
                prep_v = None if t.odd else t.pair(0)
                chn = t.pair(-7) if t.odd else None
                pln = None if t.odd else t.pair(-8)
                for k in range(8):
                    if k == 1 and ln1:
                        wait(dve, bn_ready, 4 * ln1[0] + 4)
                    if k == 5 and ln2:
                        wait(dve, bn2_ready, 4 * ln2[0] + 4)
                    if k == 4 and chn:
                        own(chn[0], 2)
                    if k == 5 and chn:
                        own(chn[0], 3)
                    reduce_unit(t, k)
                    if k == 2 and t.fixed and t.i == -1 and t.odd:
                        set_up(t.r)
                    if k == 2 and t.fixed and t.i == t.r == 0:
                        dve.wait_ge(iota_ready, 4)
                        for dst, src in ((expert_n, expert_i), (region, region_i), (fill, region_i), (token, token_i), (tile_n, tile_i)):
                            dve.tensor_copy(dst[:], src[:]).then_inc(floats_ready, 1)
                    if k == 5 and t.fixed and t.i == t.r == 0:
                        dve.wait_ge(floats_ready, 5)
                    if k == 4 and t.batch(3):
                        b, bi, slot = t.batch(3)
                        par = slot % 2
                        wait(dve, av_done, 2 * b + 2)
                        wait(dve, x1_ready, b - 1)
                        dve.transpose(att[par][:].rearrange("p g m d -> p (g m) d"),
                                      ps_av[:].rearrange("p g (u m) -> p g m u", m=8)).then_inc(att_ready, 1)
                    if k == 5 and t.batch(3):
                        wait(dve, att_ready, b + 1)
                        dve.reciprocal(rden[slot % 2][:], att[slot % 2][:, :, :, DK]).then_inc(rden_ready, 1)
                    if k == 0 and ln1:
                        n, par = ln1
                        dve.wait_ge(x_loaded[par], 16 * (same_parity(t, 4) + 1))
                        for c in range(4):
                            dve.bn_stats(bn[:, c, :], tile_of(n, c)).then_inc(bn_ready, 1)
                    if k == 1 and ln1:
                        n, par = ln1
                        for c in range(4):
                            last = dve.bn_aggr(mv[:, c, :], bn[:, c, :])
                        last.then_inc(mv_ready, 1)
                        wait(dve, mv_ready, n + 1)
                        wait(dve, shift_ready, n)
                        dve.tensor_scalar(neg_mean[:], mv[:, :, 0], -1.0, None, ALU.mult)
                        dve.tensor_scalar(var_e[:], mv[:, :, 1], 1.0 + EPS, EPS * EPS, ALU.mult, ALU.add).then_inc(var_ready, 1)
                    if k == 2 and ln2:
                        n = ln2[0]
                        wait(dve, x1_ready, 2 * n + 2)
                        for c in range(4):
                            dve.bn_stats(bn2[:, c, :], tile_of(n, c)).then_inc(bn2_ready, 1)
                    if k == 5 and ln2:
                        n = ln2[0]
                        for c in range(4):
                            last = dve.bn_aggr(mv2[:, c, :], bn2[:, c, :])
                        last.then_inc(mv2_ready, 1)
                        wait(dve, mv2_ready, n + 1)
                        wait(dve, shift2_ready, n)
                        dve.tensor_scalar(neg_mean2[:], mv2[:, :, 0], -1.0, None, ALU.mult)
                        dve.tensor_scalar(var2[:], mv2[:, :, 1], EPS, None, ALU.add).then_inc(var2_ready, 1)
                    if k == 6 and prep_v:
                        n, par = prep_v
                        wait(dve, v_proj, n + 1)
                        wait(dve, av_done, 4 * n - 4)
                        dve.tensor_tensor(v_aug[par][:, :, :, 0:DK],
                                          ps_mv[:].rearrange("p (c h d) -> p c h d", c=4, h=H),
                                          bv_s[:].rearrange("p (o h d) -> p o h d", o=1, h=H).to_broadcast([P, 4, H, DK]),
                                          ALU.add).then_inc(v_ready, 1)
                    if chn:
                        choose(k, *chn)
                    if pln:
                        place(k, *pln, t)

            periods(dve, body)
            made = [0]

            def make(ins):
                made[0] += 1
                ins.then_inc(tabling, 1)
                dve.wait_ge(tabling, made[0])

            def over_tiles(a):
                return a[:].unsqueeze(1).to_broadcast([P, FFN_TILES, E])

            dve.wait_ge(filled, B // 2)
            make(dve.tensor_tensor(total[:], fill[:], region[:], ALU.subtract))
            make(dve.tensor_scalar(tiles_i[:, 0, :], total[:], float(SLOTS - 1), None, ALU.add))
            make(dve.tensor_scalar(tiles_i[:, 1, :], tiles_i[:, 0, :], SLOTS.bit_length() - 1, None, ALU.arith_shift_right))
            make(dve.tensor_copy(tiles_f[:], tiles_i[:, 1, :]))
            make(dve.tensor_tensor_scan(tiles_end[:], ones_e[:], tiles_f[:], 0.0, ALU.mult, ALU.add))
            make(dve.tensor_tensor(passed[:], over_tiles(tiles_end),
                                   tile_n[:].unsqueeze(2).to_broadcast([P, FFN_TILES, E]), ALU.is_le))
            make(dve.tensor_reduce(tile_e[:], passed[:], AX.X, ALU.add))
            make(dve.tensor_tensor(passed_end[:], passed[:], over_tiles(tiles_end), ALU.mult))
            make(dve.tensor_reduce(tile_start[:], passed_end[:], AX.X, ALU.max))
            make(dve.tensor_tensor(tile_k[:], tile_n[:], tile_start[:], ALU.subtract))
            make(dve.tensor_scalar(tile_start[:], tile_e[:], float(REGION), None, ALU.mult))
            make(dve.scalar_tensor_tensor(out=tile_row[:], in0=tile_k[:], scalar=float(SLOTS), in1=tile_start[:],
                                          op0=ALU.mult, op1=ALU.add))
            make(dve.tensor_scalar(table[:, :, 0], tile_row[:], float(E * REGION), None, ALU.min))
            make(dve.tensor_scalar(table[:, :, 1], tile_e[:], float(E - 1), None, ALU.min))
            dve.tensor_copy(pad_start[:], fill[:]).then_inc(table_ready, 1)
            dve.wait_ge(table_ready, 1)

            def lo_part(lo, x, hi, s):
                dve.tensor_tensor(lo, x, hi.bitcast(F32), ALU.subtract).then_inc(s, 1)

            def hi_part(hi, x, loaded, value, s):
                dve.wait_ge(loaded, value)
                dve.tensor_copy(hi, x).then_inc(s, 1)

            def hidden_lo(t, f):
                if t.tile(0):
                    n, i, r = t.tile(0)
                    dve.wait_ge(h_hi_ready, 4 * n + f + 1)
                    lo_part(h_lo[r % 2][f], h_f32[f % 2], h_hi[r % 2][f], h_lo_ready)

            def body_b(t):
                if t.tile(-2):
                    n, i, r = t.tile(-2)
                    dve.wait_ge(o_psum, n + 1)
                    if since(n, 2):
                        dve.wait_ge(o_tok_psum, n - 1)
                    dve.tensor_scalar(oT[r % 2], ps_o[r % 2], b_cur[r][:, FC:FC + 1], None, ALU.add).then_inc(oT_ready, 1)
                if t.tile(1):
                    n, i, r = t.tile(1)
                    hi_part(w1_hi[r % 2], w1_raw[r % 2], w1_loaded[r % 2], loads(i, r, 2), w1_hi_ready)
                hidden_lo(t, 0)
                if t.tile(1):
                    n, i, r = t.tile(1)
                    dve.wait_ge(y_hi_ready, n + 1)
                    lo_part(y_lo[r % 2], ps_y, y_hi[r % 2], y_lo_ready)
                if t.tile(0):
                    n, i, r = t.tile(0)
                    hi_part(w2_hi[r % 2], w2_raw[r % 2], w2_loaded[r % 2], loads(i, r, 2), w2_hi_ready)
                hidden_lo(t, 1)
                if t.tile(1):
                    n, i, r = t.tile(1)
                    dve.wait_ge(w1_hi_ready, n + 1)
                    lo_part(w1_lo[r % 2], w1_raw[r % 2], w1_hi[r % 2], w1_lo_ready)
                if t.tile(-2):
                    n, i, r = t.tile(-2)
                    dve.wait_ge(o_tok_psum, n + 1)
                    if since(n, 2):
                        dve.wait_ge(added[r % 2], 64 * (i * 2 + r // 2))
                    dve.tensor_tensor(res[r % 2].rearrange("p (c d) -> p c d", d=D),
                                      ps_t.rearrange("p (c d) -> p c d", d=D),
                                      gate_row[r][:, :, 0:1].to_broadcast([P, SLOTS // P, D]),
                                      ALU.mult).then_inc(res_ready, 1)
                hidden_lo(t, 2)
                if t.tile(-1):
                    n, i, r = t.tile(-1)
                    if since(n, 4):
                        dve.wait_ge(added[r % 2], 64 * (i * 2 + r // 2 - 1))
                    dve.wait_ge(y_loaded[r], loads(i, r, 4))
                    dve.tensor_copy(gate_row[r][:, :, 0], y_tile[r][:, :, D])
                    dve.tensor_copy(gate_row[r][:, :, 1].bitcast(I32), y_tile[r][:, :, D + 1].bitcast(I32)).then_inc(gate_row_ready, 1)
                hidden_lo(t, 3)

            steps(dve, body_b)


_INS = ['L0_attn_x', 'L0_attn_Wq', 'L0_attn_bq', 'L0_attn_Wk', 'L0_attn_bk', 'L0_attn_Wv', 'L0_attn_bv', 'L0_attn_gamma', 'L0_attn_beta',
        'L0_ffn_centroids', 'L0_ffn_W1', 'L0_ffn_b1', 'L0_ffn_W2', 'L0_ffn_b2']


def kernel(**inputs):
    import numpy as _np
    import concourse.bacc as _bacc
    from concourse import mybir as _mybir
    from concourse.bass_utils import run_bass_kernel_spmd as _run

    nc = _bacc.Bacc("TRN2", target_bir_lowering=False, num_devices=1)
    arrays, args = {}, []
    for name in _INS:
        a = _np.ascontiguousarray(inputs[name])
        arrays[f"in_{name}_dram"] = a
        args.append(nc.dram_tensor(f"in_{name}_dram", a.shape, _mybir.dt.from_np(a.dtype), kind="ExternalInput").ap())
    args.append(nc.dram_tensor("out_0_dram", (B, S, D), F32, kind="ExternalOutput").ap())
    build(nc, *args)
    r = _run(nc, [arrays], core_ids=[0])
    return r.results[0]["out_0_dram"]
```
